# Optimizing a Trainium2 kernel written in Bass

```python
import numpy as np
import jax
import jax.numpy as jnp

def _softmax(x, axis=-1):
    return jax.nn.softmax(x, axis=axis)

def _gelu(x):
    return jax.nn.gelu(x, approximate=True)

def _silu(x):
    return jax.nn.silu(x)

def _sigmoid(x):
    return jax.nn.sigmoid(x)

def _layernorm(x, axis=-1, eps=1e-05):
    m = jnp.mean(x, axis=axis, keepdims=True)
    v = jnp.var(x, axis=axis, keepdims=True)
    return (x - m) / jnp.sqrt(v + eps)

def _scatter_add(tgt, idx, src, axis=0):
    return tgt.at[idx].add(src)

def _segment_sum(src, seg, n):
    return jax.ops.segment_sum(src, seg, n)
kernel_name = 'mk_macaron_d1_jaxref_r8_4dd77e'

def setup_inputs(seed: int=0):
    np.random.seed(seed)
    _w = jnp.asarray

    def _L0_attn_setup():
        import jax, jax.numpy as jnp
        import numpy as np
        from math import sqrt
        HEADS = 16
        MODEL_DIM = 128
        DIM_PER_HEAD = MODEL_DIM // HEADS
        MAX_REL_POS = 32
        ROPE_BASE = 10000.0
        NEG_INF = -1e+18

        def _rope_cos_sin(seq_len, dim):
            inv_freq = 1.0 / ROPE_BASE ** (jnp.arange(0, dim, 2, dtype=jnp.float32) / dim)
            t = jnp.arange(seq_len, dtype=jnp.float32)
            ang = jnp.outer(t, inv_freq)
            return (jnp.cos(ang), jnp.sin(ang))

        def _apply_rotary_interleave(x, cos, sin):
            B, H, L, D = x.shape
            x_ = x.reshape(B, H, L, D // 2, 2)
            xe, xo = (x_[..., 0], x_[..., 1])
            c = cos[None, None, :, :]
            s = sin[None, None, :, :]
            oe = xe * c - xo * s
            oo = xe * s + xo * c
            return jnp.stack([oe, oo], axis=-1).reshape(B, H, L, D)
        key = jax.random.key(seed)
        ks = jax.random.split(key, 6)
        B, L = (2, 128)
        scale = 0.02
        x = jax.random.normal(ks[0], (B, L, MODEL_DIM), dtype=jnp.float32)
        w_q = jax.random.normal(ks[1], (MODEL_DIM, MODEL_DIM), dtype=jnp.float32) * scale
        w_k = jax.random.normal(ks[2], (MODEL_DIM, MODEL_DIM), dtype=jnp.float32) * scale
        w_v = jax.random.normal(ks[3], (MODEL_DIM, MODEL_DIM), dtype=jnp.float32) * scale
        w_o = jax.random.normal(ks[4], (MODEL_DIM, MODEL_DIM), dtype=jnp.float32) * scale
        rel_emb = jax.random.normal(ks[5], (2 * MAX_REL_POS + 1, DIM_PER_HEAD), dtype=jnp.float32) * scale
        return {'x': x, 'w_q': w_q, 'w_k': w_k, 'w_v': w_v, 'w_o': w_o, 'rel_emb': rel_emb}
    _L0_attn_in = _L0_attn_setup()

    def _L0_ffn_setup():
        import jax, jax.numpy as jnp
        import numpy as np
        NUM_EXPERTS = 8
        HIDDEN = 128
        FFN = 512
        BATCH = 2
        SEQ = 256
        key = jax.random.key(seed)
        k_x, k_g, k_u, k_d = jax.random.split(key, 4)
        scale_in = 1.0 / np.sqrt(HIDDEN)
        scale_mid = 1.0 / np.sqrt(FFN)
        return {'hidden_states': jax.random.normal(k_x, (BATCH, SEQ, HIDDEN), dtype=jnp.float32), 'Wg': jax.random.normal(k_g, (NUM_EXPERTS, HIDDEN, FFN), dtype=jnp.float32) * scale_in, 'Wu': jax.random.normal(k_u, (NUM_EXPERTS, HIDDEN, FFN), dtype=jnp.float32) * scale_in, 'Wd': jax.random.normal(k_d, (NUM_EXPERTS, FFN, HIDDEN), dtype=jnp.float32) * scale_mid}
    _L0_ffn_in = _L0_ffn_setup()
    _d = {'L0_attn_x': _L0_attn_in['x'], 'L0_attn_w_q': _L0_attn_in['w_q'], 'L0_attn_w_k': _L0_attn_in['w_k'], 'L0_attn_w_v': _L0_attn_in['w_v'], 'L0_attn_w_o': _L0_attn_in['w_o'], 'L0_attn_rel_emb': _L0_attn_in['rel_emb'], 'L0_ffn_Wg': _L0_ffn_in['Wg'], 'L0_ffn_Wu': _L0_ffn_in['Wu'], 'L0_ffn_Wd': _L0_ffn_in['Wd']}
    _x0 = _d['L0_attn_x']
    _d['L0_attn_x'] = jax.random.normal(jax.random.fold_in(jax.random.key(seed), 1), (8, 512, 128), dtype=_x0.dtype)
    del _x0
    return _d

def reference(L0_attn_x, L0_attn_w_q, L0_attn_w_k, L0_attn_w_v, L0_attn_w_o, L0_attn_rel_emb, L0_ffn_Wg, L0_ffn_Wu, L0_ffn_Wd):

    def _L0_attn_ref(x, w_q, w_k, w_v, w_o, rel_emb):
        import jax, jax.numpy as jnp
        import numpy as np
        from math import sqrt
        HEADS = 16
        MODEL_DIM = 128
        DIM_PER_HEAD = MODEL_DIM // HEADS
        MAX_REL_POS = 32
        ROPE_BASE = 10000.0
        NEG_INF = -1e+18

        def _rope_cos_sin(seq_len, dim):
            inv_freq = 1.0 / ROPE_BASE ** (jnp.arange(0, dim, 2, dtype=jnp.float32) / dim)
            t = jnp.arange(seq_len, dtype=jnp.float32)
            ang = jnp.outer(t, inv_freq)
            return (jnp.cos(ang), jnp.sin(ang))

        def _apply_rotary_interleave(x, cos, sin):
            B, H, L, D = x.shape
            x_ = x.reshape(B, H, L, D // 2, 2)
            xe, xo = (x_[..., 0], x_[..., 1])
            c = cos[None, None, :, :]
            s = sin[None, None, :, :]
            oe = xe * c - xo * s
            oo = xe * s + xo * c
            return jnp.stack([oe, oo], axis=-1).reshape(B, H, L, D)
        B, L, _ = x.shape

        def shape(t):
            return t.reshape(B, L, HEADS, DIM_PER_HEAD).transpose(0, 2, 1, 3)
        q = shape(x @ w_q.T)
        k = shape(x @ w_k.T)
        v = shape(x @ w_v.T)
        cos, sin = _rope_cos_sin(L, DIM_PER_HEAD)
        q = _apply_rotary_interleave(q, cos, sin)
        k = _apply_rotary_interleave(k, cos, sin)
        q = q / sqrt(DIM_PER_HEAD)
        scores = jnp.einsum('bhqd,bhkd->bhqk', q, k)
        pos = jnp.arange(L)
        rel_idx = jnp.clip(pos[None, :] - pos[:, None], -MAX_REL_POS, MAX_REL_POS) + MAX_REL_POS
        rel = rel_emb[rel_idx]
        scores = scores + jnp.einsum('bhqd,qkd->bhqk', q, rel)
        causal = jnp.tril(jnp.ones((L, L), dtype=bool))
        scores = jnp.where(causal[None, None], scores, NEG_INF)
        attn = jax.nn.softmax(scores, axis=-1)
        ctx = jnp.einsum('bhqk,bhkd->bhqd', attn, v)
        ctx = ctx + jnp.einsum('bhqk,qkd->bhqd', attn, rel)
        out = ctx.transpose(0, 2, 1, 3).reshape(B, L, MODEL_DIM) @ w_o.T
        return out

    def _L0_ffn_ref(hidden_states, Wg, Wu, Wd):
        import jax, jax.numpy as jnp
        import numpy as np
        NUM_EXPERTS = 8
        HIDDEN = 128
        FFN = 512
        BATCH = 2
        SEQ = 256
        B, S, H = hidden_states.shape
        x = hidden_states.reshape(-1, H)

        def expert_step(acc, w):
            wg, wu, wd = w
            h = jax.nn.silu(x @ wg) * (x @ wu)
            return (acc + h @ wd, None)
        acc, _ = jax.lax.scan(expert_step, jnp.zeros_like(x), (Wg, Wu, Wd))
        return acc.reshape(B, S, H)
    x = L0_attn_x
    x = x + 0.5 * _L0_ffn_ref(_layernorm(x, axis=-1), L0_ffn_Wg, L0_ffn_Wu, L0_ffn_Wd)
    x = x + _L0_attn_ref(_layernorm(x, axis=-1), L0_attn_w_q, L0_attn_w_k, L0_attn_w_v, L0_attn_w_o, L0_attn_rel_emb)
    x = x + 0.5 * _L0_ffn_ref(_layernorm(x, axis=-1), L0_ffn_Wg, L0_ffn_Wu, L0_ffn_Wd)
    return x

_drawn_inputs = setup_inputs


def setup_inputs(seed=0):
    import zlib

    import numpy as np

    out = dict(_drawn_inputs(seed))
    spreads = {}
    factors = {'L0_attn_w_q': 8.0,
     'L0_attn_w_k': 8.0,
     'L0_attn_w_v': 8.0,
     'L0_attn_w_o': 8.0,
     'L0_attn_rel_emb': 8.0}
    for name, (base, spread) in spreads.items():
        noise = np.random.default_rng([zlib.crc32(name.encode()), seed]).standard_normal(out[name].shape)
        drawn = base * np.exp(spread * noise) if base else spread * noise
        out[name] = jnp.asarray(drawn.astype(out[name].dtype))
    for name, factor in factors.items():
        out[name] = (out[name] * factor).astype(out[name].dtype)
    return out
```

```python
import concourse.bass as bass
from concourse import mybir
from contextlib import ExitStack


def macaron_kernel(nc, x_d, wg_d, wu_d, wd_d, watt_d, rel_g_d, rel_g0_d, rel_c_d, rel_c0_d,
                   rel_k0_d, rel_v0_d, cos_d, sin_d, window_d, ident_d, lanes_d, out_d):
    F32 = mybir.dt.float32
    F32R = mybir.dt.float32r
    ALU = mybir.AluOpType
    ACT = mybir.ActivationFunctionType
    AX = mybir.AxisListType

    P = 128
    B, L, D = x_d.shape
    E, _, F = wg_d.shape
    FC = F // P
    CH = E * FC
    NT = L // P
    H = 16
    DH = D // H
    R = 32
    HQ = 4
    HG = H // HQ
    W = P + R
    NU = H * NT
    QSCALE = float(DH) ** -0.5
    EPS = 1e-5
    LAG = 2
    TILE = P * W
    HI, LO = 0, 1

    zwin_h = nc.dram_tensor("rel_window_scratch", [H * NT * TILE], F32, kind="Internal")
    pwin_h = nc.dram_tensor("prob_window_scratch", [H * NT * TILE], F32, kind="Internal")
    qk_h = nc.dram_tensor("qk_scratch", [4, P, L], F32, kind="Internal")
    zwin_t, pwin_t, qk_t = zwin_h.ap().tensor, pwin_h.ap().tensor, qk_h.ap().tensor

    ctx = ExitStack()
    with ctx:
        def sb(name, shape, dt=F32):
            return ctx.enter_context(nc.sbuf_tensor(name, shape, dt))

        def pb(name, shape):
            return ctx.enter_context(nc.psum_tensor(name, shape, F32))

        def sem(name):
            return ctx.enter_context(nc.semaphore(name))

        wg = sb("wg", [P, 2, E, F], F32R)
        wu = sb("wu", [P, 2, E, F], F32R)
        wd = sb("wd", [P, 2, E, F], F32R)
        watt = sb("watt", [P, 2, 6, P], F32R)
        WQ, WQS, WK, WKS, WV, WO = range(6)
        x0 = sb("x0", [P, L])
        x1 = sb("x1", [P, L])
        x2 = sb("x2", [P, L])
        xn = sb("xn", [P, L])
        xt1 = sb("xt1", [P, 2, L], F32R)
        xt2 = sb("xt2", [P, 2, L], F32R)
        acc_t = sb("acc_t", [P, L])
        out_s = sb("out_s", [P, L])
        th = sb("th", [P, 2, L])
        hid = sb("hid", [P, 2, L])
        hid_hi = sb("hid_hi", [P, 2, L], F32R)
        hid_lo = sb("hid_lo", [P, 2, L], F32R)
        cos_s = sb("cos_s", [P, L])
        sin_s = sb("sin_s", [P, L])
        qq = sb("qq", [P, HG, L], F32R)
        kk = sb("kk", [P, HG, L], F32R)
        v_s = sb("v_s", [P, NT, P])
        rel_win = sb("rel_win", [P, 3, NT, W])
        g_a = sb("g_a", [P, NT, H, R])
        probs = sb("probs", [P, 2, R + NT * L])
        probs_t = sb("probs_t", [P, 2, L])
        band_t = sb("band_t", [P, L])
        ctx_s = sb("ctx_s", [P, L])
        ctx_t = sb("ctx_t", [P, 2, L], F32R)
        negmax = sb("negmax", [P, NU])
        denom = sb("denom", [P, NU])
        rdenom = sb("rdenom", [P, NU])
        rel_g = sb("rel_g", [P, P], F32R)
        rel_c = sb("rel_c", [P, R])
        rel_k0 = sb("rel_k0", [P, 1])
        rel_v0 = sb("rel_v0", [P, P])
        ident = sb("ident", [P, P])
        lanes = sb("lanes", [P, 2])
        stats = sb("stats", [P, NT, 6])
        moments = sb("moments", [P, NT, 2])
        var_eps = sb("var_eps", [P, NT])
        rstd = sb("rstd", [P, NT])
        minus_half = sb("minus_half", [P, NT])
        eps = sb("eps", [P, NT])
        settled = sb("settled", [P, 1])

        rope = [probs[:, 0, R + i * L:R + (i + 1) * L] for i in range(4)]
        Q1, Q2, K1, K2 = rope
        qk = probs[:, 1, R:].rearrange("p (c l) -> p c l", c=4)
        qk_r = qk.bitcast(F32R)
        stage = [probs[:, i, R:R + 3 * F] for i in range(2)]
        raw_att = g_a[:, :, :, :].rearrange("p a b c -> p (a b c)")[:, 0:6 * P]
        raw_rel = g_a[:, :, :, :].rearrange("p a b c -> p (a b c)")[:, 6 * P:6 * P + 2 * P + 2 * R]
        window = rel_win[:, 0, 0, :]

        gate = [pb(f"gate{i}", [P, L]) for i in range(2)]
        up = [pb(f"up{i}", [P, L]) for i in range(2)]
        acc = pb("acc", [P, L])
        work = [pb(f"work{i}", [P, L]) for i in range(2)]
        ctx_p = pb("ctx_p", [P, L])

        s_w = [sem(f"expert_loaded{i}") for i in range(2)]
        s_wsplit_hi = sem("expert_hi")
        s_wsplit_lo = sem("expert_up_lo")
        s_wsplit_dlo = sem("expert_down_lo")
        s_const = sem("constants_loaded")
        s_win = sem("window_loaded")
        s_half = sem("exponent_set")
        s_pad = sem("pads_zeroed")
        s_att_hi = sem("att_weights_hi")
        s_att_lo = sem("att_weights_lo")
        s_rel = sem("rel_prepared")
        s_gate = sem("gate_ready")
        s_up = sem("up_ready")
        s_tanh = sem("tanh_ready")
        s_act = sem("gated_ready")
        s_hid = sem("hid_ready")
        s_hhi = sem("hid_hi_ready")
        s_hlo = sem("hid_lo_ready")
        s_down = sem("down_done")
        s_acc = sem("acc_copied")
        s_ftok = sem("ffn_tokens")
        s_sum = sem("residual_summed")
        s_st = sem("stats_done")
        s_mom = sem("moments_ready")
        s_ve = sem("var_eps_ready")
        s_rstd = sem("rstd_ready")
        s_xn = sem("xn_ready")
        s_xnt = sem("xn_transposed")
        s_xhi = sem("xt_hi_ready")
        s_xlo = sem("xt_lo_ready")
        s_proj = sem("projected")
        s_rope = sem("rope_step")
        s_qkhi = sem("qk_hi_ready")
        s_qklo = sem("qk_lo_ready")
        s_v = sem("v_ready")
        s_qkst = sem("qk_stored")
        s_qkld = sem("qk_loaded")
        s_g = sem("qrel_done")
        s_gev = sem("qrel_copied")
        s_gst = sem("qrel_stored")
        s_z = [sem(f"window_of_head_loaded{i}") for i in range(3)]
        s_sc = sem("scores_ready")
        s_zadd = sem("window_added")
        s_max = sem("max_ready")
        s_exp = sem("probs_ready")
        s_pt = sem("probs_transposed")
        s_ptc = sem("probs_t_copied")
        s_pv = sem("pv_done")
        s_pst = [sem(f"prob_window_stored{i}") for i in range(2)]
        s_band = sem("band_loaded")
        s_bt = sem("band_transposed")
        s_btc = sem("band_t_copied")
        s_crel = sem("ctx_rel_ready")
        s_cc = sem("ctx_copied")
        s_cn = sem("ctx_step")
        s_ct = sem("ctx_transposed")
        s_chi = sem("ctx_t_hi")
        s_clo = sem("ctx_t_lo")
        s_o = sem("attention_out")
        s_x2 = sem("attention_summed")
        s_x = sem("x_loaded")
        s_out = sem("dram_filled_then_outputs_stored")

        x_v = x_d.rearrange("b (t p) d -> b p t d", p=P)
        out_v = out_d.rearrange("b (t p) d -> b p t d", p=P)

        def wait(eng, semaphore, value):
            if not (isinstance(value, int) and value <= 0):
                eng.wait_ge(semaphore, value)

        NORM2 = ["acc1", "sum1", "ln2a", "ln2b", "ln2c"]
        PROJECT = ["proj1", "proj2", "proj3"]
        NORM1 = ["ln1a", "ln1b", "ln1c"]
        QREL = ["qrel1", "qrel2"]
        OUTPUT = ["acc2", "sum2"]
        CONTEXT = ["ctx0", "ctx1", "ctx2", "ctx3", "ctx4", "ctx5", "ctx6", "ctx7", "ln3a", "ln3b", "ln3c"]

        def plan(slots, ahead, names, first, last, out_at):
            pieces = [[] for _ in range(slots + 1)]
            for i, name in enumerate(names):
                pieces[LAG - 1 + i].append((name, 0))
            steps = NU + 2
            for u in range(steps):
                pieces[first + u * (last - first) // steps].append(("unit", u))
            if out_at == slots:
                pieces[slots] += [("acc2", 0), ("sum2", NU)]
            elif out_at is not None:
                pieces[out_at].append(("acc2", 0))
                for slot in pieces[out_at + 1:]:
                    even = [i for i, (_, u) in enumerate(slot) if u % 2 == 0]
                    if even:
                        u = slot[even[0]][1]
                        slot[even[0]:even[0] + 1] = [("sum2", u), ("unit_after_sum2", u)]
                        break
            for i, name in enumerate(CONTEXT):
                pieces[min(last + i, slots)].append((name, 0))
            return [(name, 0) for name in ahead], pieces

        FULL_STEP = plan(2 * CH, [], NORM2 + PROJECT + NORM1 + QREL, 16, 2 * CH - len(CONTEXT), CH + LAG - 1)
        FIRST_STEP = plan(CH, NORM2 + PROJECT + NORM1 + QREL, [], 2, CH, None)
        LAST_STEP = plan(CH, [], NORM2 + PROJECT + QREL, 13, CH, CH)

        def ln_index(name, t):
            after_ln2 = 1 if not isinstance(t, int) or t < B - 1 else 0
            return 3 * t + 1 + {"ln2": 0, "ln1": 1, "ln3": 1 + after_ln2}[name[:3]]

        def sum_index(name, t):
            first = 2 * t - 1 if not isinstance(t, int) or t > 0 else 0
            return {"1": first, "2": 2 * t}[name[-1]]

        def before(n_pass, k, j):
            return (n_pass, k - j) if k >= j else (n_pass - 1, CH + k - j)

        def whole_program(eng, chunk, flush, run, prologue, split_expert):
            prologue()
            split_expert(0)
            for k in range(CH):
                chunk(0, k, False, 0, k)
                if k % FC == 0 and k // FC + 1 < E:
                    split_expert(k // FC + 1)
            flush(0)
            ahead, pieces = FIRST_STEP
            for name, arg in ahead:
                run(name, arg, 0)
            for k in range(CH):
                chunk(1, k, False, ln_index("ln1", 0), k)
                for name, arg in pieces[k]:
                    run(name, arg, 0)
            for name, arg in pieces[CH]:
                run(name, arg, 0)
            with eng.Fori(1, B - 1) as t:
                ahead, pieces = FULL_STEP
                for k in range(CH):
                    chunk(2 * t, k, True, 3 * t, CH)
                    for name, arg in pieces[k]:
                        run(name, arg, t)
                for k in range(CH):
                    chunk(2 * t + 1, k, False, ln_index("ln1", t), CH)
                    for name, arg in pieces[CH + k]:
                        run(name, arg, t)
                for name, arg in pieces[2 * CH]:
                    run(name, arg, t)
            t = B - 1
            ahead, pieces = LAST_STEP
            for k in range(CH):
                chunk(2 * t, k, True, 3 * t, CH)
                for name, arg in pieces[k]:
                    run(name, arg, t)
            flush(2 * t)
            for name, arg in pieces[CH]:
                run(name, arg, t)
            for k in range(CH):
                chunk(2 * B - 1, k, True, ln_index("ln3", t), k)
            flush(2 * B - 1)
            run("acclast", 0, B)
            run("sumlast", 0, B)

        block = ctx.enter_context(nc.Block())

        @block.sync
        def _(sp):
            def no_chunk(n_pass, k, second, ln, led):
                pass

            def no_split(e):
                pass

            def no_flush(n_pass):
                pass

            def prologue():
                sp.dma_start(x0[:, :].rearrange("p (t d) -> p t d", t=NT), x_v[0]).then_inc(s_x, 16)
                for i, (dst, src) in enumerate(((ident[:, :], ident_d), (window, window_d),
                                                (raw_att, watt_d), (cos_s[:, :], cos_d),
                                                (sin_s[:, :], sin_d), (rel_k0[:, :], rel_k0_d),
                                                (rel_v0[:, :], rel_v0_d), (lanes[:, :], lanes_d),
                                                (raw_rel[:, 0:P], rel_g_d), (raw_rel[:, P:2 * P], rel_g0_d),
                                                (raw_rel[:, 2 * P:2 * P + R], rel_c_d),
                                                (raw_rel[:, 2 * P + R:], rel_c0_d))):
                    if i == 2:
                        for e in range(2):
                            load_expert(e)
                    sp.dma_start(dst, src).then_inc(s_win if i == 1 else s_const, 16)
                for e in range(2, E):
                    sp.wait_ge(s_wsplit_hi, e - 1)
                    sp.wait_ge(s_wsplit_lo, e - 1)
                    sp.wait_ge(s_wsplit_dlo, e - 1)
                    load_expert(e)
                sp.wait_ge(s_win, 16)
                sp.dma_start(bass.AP(zwin_t, 0, [[W, P], [TILE, H * NT], [1, W]]),
                             window[:, None, :].to_broadcast([P, H * NT, W])).then_inc(s_out, 16)
                sp.wait_ge(s_out, 16)

            def load_expert(e):
                dst = stage[e % 2]
                sp.dma_start(dst[:, 0:F], wg_d[e]).then_inc(s_w[e % 2], 16)
                sp.dma_start(dst[:, F:2 * F], wu_d[e]).then_inc(s_w[e % 2], 16)
                sp.dma_start(dst[:, 2 * F:3 * F].rearrange("p (c d) -> p c d", c=FC),
                             wd_d[e].rearrange("(c p) d -> p c d", p=P)).then_inc(s_w[e % 2], 16)

            def load_window(h, t):
                if h >= 3:
                    sp.wait_ge(s_zadd, NU * t + NT * (h - 2))
                sp.dma_start(rel_win[:, h % 3, :, :],
                             bass.AP(zwin_t, h * NT * TILE, [[W, P], [TILE, NT], [1, W]])).then_inc(s_z[h % 3], 16)

            def run(name, arg, t):
                if name == "sum1" and (not isinstance(t, int) or t < B - 1):
                    sp.wait_ge(s_sum, sum_index("sum1", t) + 1)
                    sp.dma_start(x0[:, :].rearrange("p (t d) -> p t d", t=NT),
                                 x_v[t + 1]).then_inc(s_x, 16)
                if name == "proj3":
                    sp.wait_ge(s_qkhi, 2 * t + 2)
                    sp.wait_ge(s_qklo, 2 * t + 2)
                    sp.dma_start(qk_h.ap().rearrange("c p l -> p c l"), qk[:, :, :]).then_inc(s_qkst, 16)
                    sp.wait_ge(s_qkst, 16 * (t + 1))
                    for a in range(HQ):
                        for c in range(4):
                            rows = slice(32 * a + DH * c, 32 * a + DH * (c + 1))
                            for dst, part in ((qq, c // 2), (kk, 2 + c % 2)):
                                sp.dma_start(dst[rows, :, :].bitcast(F32).rearrange("p g l -> p (g l)"),
                                             bass.AP(qk_t, part * P * L + a * HG * L, [[H * L, DH], [1, HG * L]])
                                             ).then_inc(s_qkld, 16)
                if name == "qrel2":
                    for i in range(NT):
                        sp.wait_ge(s_gev, NT * t + i + 1)
                        sp.dma_start(bass.AP(zwin_t, i * TILE + 1, [[W + 1, P], [NT * TILE, H], [1, R]]),
                                     g_a[:, i, :, :]).then_inc(s_gst, 16)
                    sp.wait_ge(s_gst, 16 * NT * (t + 1))
                    for h in range(2):
                        load_window(h, t)
                if name.startswith("unit") and arg % NT == 0 and arg // NT + 2 < H:
                    load_window(arg // NT + 2, t)
                if name.startswith("unit") and arg >= NT and arg % NT == 1:
                    h = arg // NT - 1
                    if h < H:
                        sp.wait_ge(s_exp, NU * t + NT * (h + 1))
                        sp.dma_start(bass.AP(pwin_t, h * NT * TILE, [[W, P], [TILE, NT], [1, W]]),
                                     bass.AP(probs[:, h % 2, :].tensor, probs[:, h % 2, :].offset,
                                             [list(probs[:, h % 2, :].ap[0]), [L + P, NT], [1, W]])
                                     ).then_inc(s_pst[h % 2], 16)
                        sp.wait_ge(s_pst[h % 2], 16 * (H // 2) * t + 16 * (h // 2 + 1))
                        sp.dma_start(g_a[:, :, h, :],
                                     bass.AP(pwin_t, h * NT * TILE + 1, [[W + 1, P], [TILE, NT], [1, R]])
                                     ).then_inc(s_band, 16)
                if name == "sum2":
                    sp.wait_ge(s_sum, sum_index("sum2", t) + 1)
                    sp.dma_start(out_v[t - 1], out_s[:, :].rearrange("p (t d) -> p t d", t=NT)).then_inc(s_out, 16)
                if name == "sumlast":
                    sp.wait_ge(s_sum, 2 * B)
                    sp.dma_start(out_v[B - 1], out_s[:, :].rearrange("p (t d) -> p t d", t=NT)).then_inc(s_out, 16)
                    sp.wait_ge(s_out, 16 * (B + 1))

            whole_program(sp, no_chunk, no_flush, run, prologue, no_split)

        @block.tensor
        def _(pe):
            def three(out, w_hi, w_lo, m_hi, m_lo, start=True, stop=True):
                pe.matmul(out, w_hi, m_hi, start=start, stop=False)
                pe.matmul(out, w_hi, m_lo, start=False, stop=False)
                return pe.matmul(out, w_lo, m_hi, start=False, stop=stop)

            def transposes(dst, src, n=NT):
                for i in range(n):
                    last = pe.transpose(dst[:, i * P:(i + 1) * P], src[:, i * P:(i + 1) * P], ident[:, :])
                return last

            def down(n_pass, k):
                n = CH * n_pass + k
                e, c = k // FC, k % FC
                pe.wait_ge(s_hhi, n + 1)
                pe.wait_ge(s_hlo, n + 1)
                if k == 0:
                    wait(pe, s_acc, n_pass)
                three(acc[:, :], wd[:, HI, e, c * P:(c + 1) * P], wd[:, LO, e, c * P:(c + 1) * P],
                      hid_hi[:, k % 2, :], hid_lo[:, k % 2, :],
                      start=(k == 0), stop=(k == CH - 1)).then_inc(s_down, 1)

            def chunk(n_pass, k, second, ln, led):
                n = CH * n_pass + k
                e, c = k // FC, k % FC
                xt = xt2 if second else xt1
                if isinstance(n_pass, int) and n_pass == 0 and k % FC == 0:
                    pe.wait_ge(s_wsplit_hi, e + 1)
                    pe.wait_ge(s_wsplit_lo, e + 1)
                    pe.wait_ge(s_wsplit_dlo, e + 1)
                if k == 0:
                    pe.wait_ge(s_xhi, ln + 1)
                    pe.wait_ge(s_xlo, ln + 1)
                wait(pe, s_act, n - 1)
                three(gate[k % 2][:, :], wg[:, HI, e, c * P:(c + 1) * P], wg[:, LO, e, c * P:(c + 1) * P],
                      xt[:, HI, :], xt[:, LO, :]).then_inc(s_gate, 1)
                wait(pe, s_hid, n - 1)
                three(up[k % 2][:, :], wu[:, HI, e, c * P:(c + 1) * P], wu[:, LO, e, c * P:(c + 1) * P],
                      xt[:, HI, :], xt[:, LO, :]).then_inc(s_up, 1)
                if led >= LAG:
                    down(*before(n_pass, k, LAG))

            def flush(n_pass):
                for k in range(CH - LAG, CH):
                    down(n_pass, k)

            def prologue():
                pe.wait_ge(s_const, 16 * 11)
                pe.wait_ge(s_xn, 1)
                transposes(work[1], xn).then_inc(s_xnt, 1)

            def no_split(e):
                pass

            def run(name, arg, t):
                if name[:3] == "sum":
                    j = 2 * B - 1 if name == "sumlast" else sum_index(name, t)
                    pe.wait_ge(s_acc, j + 1)
                    if name == "sum2":
                        wait(pe, s_ptc, NU * t + min(arg, NU) - 1)
                    transposes(work[0], acc_t).then_inc(s_ftok, 1)
                if name in ("ln1b", "ln2b", "ln3b"):
                    pe.wait_ge(s_xn, ln_index(name, t) + 1)
                    transposes(work[1], xn).then_inc(s_xnt, 1)
                if name == "proj1":
                    if isinstance(t, int) and t == 0:
                        pe.wait_ge(s_att_hi, 1)
                        pe.wait_ge(s_att_lo, 1)
                    pe.wait_ge(s_xhi, ln_index("ln2", t) + 1)
                    pe.wait_ge(s_xlo, ln_index("ln2", t) + 1)
                    for w, bank in ((WQ, work[0]), (WQS, ctx_p)):
                        three(bank[:, :], watt[:, HI, w, :], watt[:, LO, w, :],
                              xt1[:, HI, :], xt1[:, LO, :]).then_inc(s_proj, 1)
                if name == "proj2":
                    three(work[1][:, :], watt[:, HI, WK, :], watt[:, LO, WK, :],
                          xt1[:, HI, :], xt1[:, LO, :]).then_inc(s_proj, 1)
                    pe.wait_ge(s_rope, 6 * t + 1)
                    three(work[0][:, :], watt[:, HI, WKS, :], watt[:, LO, WKS, :],
                          xt1[:, HI, :], xt1[:, LO, :]).then_inc(s_proj, 1)
                if name == "proj3":
                    pe.wait_ge(s_rope, 6 * t + 2)
                    for i in range(NT):
                        cols = slice(i * P, (i + 1) * P)
                        last = three(ctx_p[:, cols], xt1[:, HI, cols], xt1[:, LO, cols],
                                     watt[:, HI, WV, :], watt[:, LO, WV, :])
                    last.then_inc(s_proj, 1)
                if name == "qrel1":
                    pe.wait_ge(s_qkld, 16 * 32 * (t + 1))
                    pe.wait_ge(s_rope, 6 * t + 5)
                    if isinstance(t, int) and t == 0:
                        pe.wait_ge(s_rel, 3)
                    pe.wait_ge(s_v, t + 1)
                if name in ("qrel1", "qrel2"):
                    for i in range(2):
                        bank = (work[0], ctx_p)[i]
                        tile = i + 2 * (name == "qrel2")
                        if name == "qrel2":
                            pe.wait_ge(s_gev, NT * t + i + 1)
                        for g in range(HG):
                            last = pe.matmul(bank[:, g * P:(g + 1) * P], qq[:, g, tile * P:(tile + 1) * P],
                                             rel_g[:, :], start=True, stop=True)
                        last.then_inc(s_g, 1)
                if name in ("unit", "unit_after_sum2"):
                    if name == "unit_after_sum2":
                        pe.wait_ge(s_sum, sum_index("sum2", t) + 1)
                    unit(arg, t)
                if name[:3] == "ctx":
                    context(int(name[3:]), t)

            def unit(u, t):
                if u < NU:
                    h, i = u // NT, u % NT
                    a, g = h % HQ, h // HQ
                    rows = slice(32 * a, 32 * a + 32)
                    if u == 0:
                        pe.wait_ge(s_gev, NT * t + NT)
                    if u == 1:
                        last_ln = "ln1" if not isinstance(t, int) or t < B - 1 else "ln2"
                        pe.wait_ge(s_xlo, ln_index(last_ln, t) + 1)
                    if u >= 2:
                        pe.wait_ge(s_ptc, NU * t + u - 1)
                    n = (i + 1) * P
                    pe.matmul(work[u % 2][:, 0:n], qq[rows, g, i * P:(i + 1) * P], kk[rows, g, 0:n],
                              start=True, stop=True).then_inc(s_sc, 1)
                if u >= 2:
                    h, i = (u - 2) // NT, (u - 2) % NT
                    pe.wait_ge(s_ptc, NU * t + u - 1)
                    for j in range(i + 1):
                        last = pe.matmul(ctx_p[:, i * P + h * DH:i * P + (h + 1) * DH],
                                         probs_t[:, u % 2, j * P:(j + 1) * P],
                                         v_s[:, j, h * DH:(h + 1) * DH], start=(j == 0), stop=(j == i))
                    last.then_inc(s_pv, 1)
                if 1 <= u <= NU:
                    h, i = (u - 1) // NT, (u - 1) % NT
                    pe.wait_ge(s_exp, NU * t + u)
                    row = probs[:, h % 2, R + i * L:R + (i + 1) * L]
                    transposes(work[(u - 1) % 2], row, i + 1).then_inc(s_pt, 1)

            def context(step, t):
                if 1 <= step <= HG:
                    g = step - 1
                    pe.wait_ge(s_btc, HG * t + g + 1)
                    for i in range(NT):
                        o = i * P + g * HQ * DH
                        last = pe.matmul(work[1][:, o:o + HQ * DH], band_t[:, i * P:(i + 1) * P],
                                         rel_c[:, :], start=True, stop=True)
                    last.then_inc(s_crel, 1)
                if step < HG:
                    g = step
                    if g == 0:
                        pe.wait_ge(s_band, 16 * H * (t + 1))
                        pe.wait_ge(s_ptc, NU * (t + 1))
                        if isinstance(t, int) and t == B - 1:
                            pe.wait_ge(s_sum, sum_index("sum2", t) + 1)
                    for i in range(NT):
                        last = pe.transpose(work[0][:, i * P:(i + 1) * P],
                                            g_a[:, i, g * HQ:(g + 1) * HQ, :].rearrange("p h r -> p (h r)"),
                                            ident[:, :])
                    last.then_inc(s_bt, 1)
                if step == 5:
                    pe.wait_ge(s_cn, 3 * t + 3)
                    transposes(work[0], ctx_s).then_inc(s_ct, 1)
                if step == 6:
                    pe.wait_ge(s_chi, t + 1)
                    pe.wait_ge(s_clo, t + 1)
                    for i in range(NT):
                        cols = slice(i * P, (i + 1) * P)
                        last = three(work[1][:, cols], ctx_t[:, HI, cols], ctx_t[:, LO, cols],
                                     watt[:, HI, WO, :], watt[:, LO, WO, :])
                    last.then_inc(s_o, 1)

            whole_program(pe, chunk, flush, run, prologue, no_split)

        @block.scalar
        def _(act):
            def hi(n_pass, k):
                n = CH * n_pass + k
                act.wait_ge(s_hid, n + 1)
                wait(act, s_down, n - 1)
                act.copy(hid_hi[:, k % 2, :], hid[:, k % 2, :]).then_inc(s_hhi, 1)

            def chunk(n_pass, k, second, ln, led):
                n = CH * n_pass + k
                act.wait_ge(s_gate, n + 1)
                wait(act, s_act, n - 1)
                act.activation(th[:, k % 2, :], gate[k % 2][:, :], ACT.Tanh, scale=0.5).then_inc(s_tanh, 1)
                if led >= 1:
                    hi(*before(n_pass, k, 1))

            def flush(n_pass):
                hi(n_pass, CH - 1)

            def split_expert(e):
                act.wait_ge(s_w[e % 2], 48 * (e // 2 + 1))
                act.copy(wg[:, HI, e, :], stage[e % 2][:, 0:F])
                act.copy(wu[:, HI, e, :], stage[e % 2][:, F:2 * F])
                act.copy(wd[:, HI, e, :], stage[e % 2][:, 2 * F:3 * F]).then_inc(s_wsplit_hi, 1)

            def prologue():
                act.wait_ge(s_xnt, 1)
                act.copy(xt1[:, HI, :], work[1][:, :]).then_inc(s_xhi, 1)
                act.wait_ge(s_const, 16 * 11)
                act.copy(watt[:, HI, :, :].rearrange("p a b -> p (a b)"), raw_att).then_inc(s_att_hi, 1)

            def run(name, arg, t):
                if name[:3] == "acc":
                    j = 2 * B - 1 if name == "acclast" else sum_index(name, t)
                    act.wait_ge(s_down, CH * (j + 1))
                    wait(act, s_ftok, j)
                    act.mul(acc_t[:, :], acc[:, :], 0.25).then_inc(s_acc, 1)
                if name in ("ln1c", "ln2c", "ln3c"):
                    xt = xt2 if name == "ln3c" else xt1
                    act.wait_ge(s_xnt, ln_index(name, t) + 1)
                    act.copy(xt[:, HI, :], work[1][:, :]).then_inc(s_xhi, 1)
                if name in ("proj2", "proj3"):
                    i = int(name[4]) - 2
                    act.wait_ge(s_rope, 6 * t + 3 * (i + 1))
                    act.copy(qk_r[:, 2 * i, :], (Q1, K1)[i]).then_inc(s_qkhi, 1)
                if name in ("qrel1", "qrel2"):
                    for i in range(2):
                        tile = i + 2 * (name == "qrel2")
                        act.wait_ge(s_g, NT * t + tile + 1)
                        act.copy(g_a[:, tile, :, :].rearrange("p h r -> p (h r)"),
                                 (work[0], ctx_p)[i][:, :]).then_inc(s_gev, 1)
                if name[:4] == "unit":
                    unit(arg, t)
                if name[:3] == "ctx" and int(name[3:]) < HG:
                    g = int(name[3:])
                    act.wait_ge(s_bt, HG * t + g + 1)
                    if g > 0:
                        act.wait_ge(s_crel, HG * t + g)
                    act.copy(band_t[:, :], work[0][:, :]).then_inc(s_btc, 1)
                if name == "ctx2":
                    act.wait_ge(s_pv, NU * (t + 1))
                    act.copy(ctx_s[:, :], ctx_p[:, :]).then_inc(s_cc, 1)
                if name == "ctx5":
                    act.wait_ge(s_ct, t + 1)
                    act.copy(ctx_t[:, HI, :], work[0][:, :]).then_inc(s_chi, 1)

            def unit(u, t):
                if u >= 2:
                    i = (u - 2) % NT
                    act.wait_ge(s_pt, NU * t + u - 1)
                    if u >= 4:
                        act.wait_ge(s_pv, NU * t + u - 3)
                    act.copy(probs_t[:, u % 2, 0:(i + 1) * P],
                             work[u % 2][:, 0:(i + 1) * P]).then_inc(s_ptc, 1)
                if 1 <= u <= NU:
                    h, i = (u - 1) // NT, (u - 1) % NT
                    act.wait_ge(s_max, NU * t + u)
                    if i == 0 and h >= 2:
                        act.wait_ge(s_pst[h % 2], 16 * (H // 2) * t + 16 * (h // 2))
                    if u == 1:
                        act.wait_ge(s_qkst, 16 * (t + 1))
                    c = i * H + h
                    act.activation(probs[:, h % 2, R + i * L:R + i * L + (i + 1) * P],
                                   work[(u - 1) % 2][:, 0:(i + 1) * P], ACT.Exp,
                                   bias=negmax[:, c:c + 1], accum_out=denom[:, c:c + 1]).then_inc(s_exp, 1)

            whole_program(act, chunk, flush, run, prologue, split_expert)

        @block.vector
        def _(dve):
            def chunk(n_pass, k, second, ln, led):
                n = CH * n_pass + k
                dve.wait_ge(s_tanh, n + 1)
                wait(dve, s_hlo, n - 1)
                dve.scalar_tensor_tensor(out=hid[:, k % 2, :], in0=th[:, k % 2, :], scalar=1.0,
                                         in1=gate[k % 2][:, :], op0=ALU.add, op1=ALU.mult).then_inc(s_act, 1)
                dve.wait_ge(s_act, n + 1)
                dve.wait_ge(s_up, n + 1)
                dve.tensor_tensor(hid[:, k % 2, :], hid[:, k % 2, :], up[k % 2][:, :],
                                  ALU.mult).then_inc(s_hid, 1)

            def flush(n_pass):
                pass

            def split_expert(e):
                dve.wait_ge(s_wsplit_hi, e + 1)
                dve.tensor_tensor(wd[:, LO, e, :], stage[e % 2][:, 2 * F:3 * F],
                                  wd[:, HI, e, :].bitcast(F32), ALU.subtract).then_inc(s_wsplit_dlo, 1)

            def prologue():
                dve.memset(minus_half[:, :], -0.5)
                dve.memset(eps[:, :], EPS).then_inc(s_half, 1)
                dve.memset(probs[:, :, 0:R], 0.0).then_inc(s_pad, 1)
                dve.wait_ge(s_x, 16)
                norm_a(0, x0)
                norm_b(0, x0)
                norm_c(0, xt1)
                dve.wait_ge(s_const, 16 * 11)
                dve.wait_ge(s_att_hi, 1)
                dve.tensor_tensor(watt[:, LO, :, :].rearrange("p a b -> p (a b)"), raw_att,
                                  watt[:, HI, :, :].rearrange("p a b -> p (a b)").bitcast(F32),
                                  ALU.subtract).then_inc(s_att_lo, 1)
                dve.tensor_tensor(rel_c[:, :], raw_rel[:, 2 * P:2 * P + R], raw_rel[:, 2 * P + R:],
                                  ALU.subtract)
                dve.tensor_tensor(raw_rel[:, 0:P], raw_rel[:, 0:P], raw_rel[:, P:2 * P],
                                  ALU.subtract).then_inc(s_rel, 1)
                dve.wait_ge(s_rel, 1)
                dve.tensor_copy(ctx_s[:, 0:P].bitcast(F32R), raw_rel[:, 0:P])
                dve.tensor_scalar(raw_rel[:, P:2 * P], raw_rel[:, 0:P], lanes[:, 0:1], None,
                                  ALU.mult).then_inc(s_rel, 1)
                dve.wait_ge(s_rel, 2)
                dve.scalar_tensor_tensor(out=rel_g[:, :], in0=ctx_s[:, 0:P], scalar=lanes[:, 1:2],
                                         in1=raw_rel[:, P:2 * P], op0=ALU.mult, op1=ALU.add).then_inc(s_rel, 1)

            def norm_a(m, x):
                for i in range(NT):
                    last = dve.bn_stats(stats[:, i, :], x[:, i * P:(i + 1) * P])
                last.then_inc(s_st, 1)
                dve.wait_ge(s_st, m + 1)
                dve.memset(settled[:, :], 0.0)
                for i in range(NT):
                    last = dve.bn_aggr(moments[:, i, :], stats[:, i, :])
                last.then_inc(s_mom, 1)

            def norm_b(m, x):
                dve.wait_ge(s_rstd, m + 1)
                wait(dve, s_xnt, m)
                for i in range(NT):
                    last = dve.tensor_scalar(xn[:, i * P:(i + 1) * P], x[:, i * P:(i + 1) * P],
                                             moments[:, i, 0:1], rstd[:, i:i + 1], ALU.subtract, ALU.mult)
                last.then_inc(s_xn, 1)

            def norm_c(m, xt):
                dve.wait_ge(s_xhi, m + 1)
                dve.tensor_tensor(xt[:, LO, :], work[1][:, :], xt[:, HI, :].bitcast(F32),
                                  ALU.subtract).then_inc(s_xlo, 1)

            def run(name, arg, t):
                if name == "sum1":
                    dve.wait_ge(s_ftok, sum_index(name, t) + 1)
                    dve.wait_ge(s_x, 16 * (t + 1))
                    dve.tensor_tensor(x1[:, :], work[0][:, :], x0[:, :], ALU.add).then_inc(s_sum, 1)
                if name in ("sum2", "sumlast"):
                    j = 2 * B - 1 if name == "sumlast" else sum_index(name, t)
                    dve.wait_ge(s_ftok, j + 1)
                    dve.wait_ge(s_out, 16 * t)
                    dve.tensor_tensor(out_s[:, :], work[0][:, :], x2[:, :], ALU.add).then_inc(s_sum, 1)
                if name == "ln2a":
                    dve.wait_ge(s_sum, sum_index("sum1", t) + 1)
                if name == "ln3a":
                    dve.wait_ge(s_x2, t + 1)
                if name == "ln1a":
                    dve.wait_ge(s_x, 16 * (t + 2))
                if name[:2] == "ln":
                    m = ln_index(name, t)
                    x = {"1": x0, "2": x1, "3": x2}[name[2]]
                    if name[3] == "a":
                        norm_a(m, x)
                    if name[3] == "b":
                        norm_b(m, x)
                    if name[3] == "c":
                        norm_c(m, xt2 if name[2] == "3" else xt1)
                if name in ("proj1", "proj2"):
                    rotate(int(name[4]) - 1, t)
                if name == "proj3":
                    dve.wait_ge(s_proj, 5 * t + 5)
                    dve.tensor_tensor(v_s[:, :, :], ctx_p[:, :].rearrange("p (a b) -> p a b", a=NT),
                                      rel_v0[:, None, :].to_broadcast([P, NT, P]), ALU.add).then_inc(s_v, 1)
                if name[:4] == "unit" and arg < NU:
                    u, h, i = arg, arg // NT, arg % NT
                    c = i * H + h
                    lo = R if i == 0 else 0
                    win = work[u % 2][:, i * P - R + lo:(i + 1) * P]
                    dve.wait_ge(s_sc, NU * t + u + 1)
                    if i == 0:
                        loads = len(range(h % 3, H, 3))
                        dve.wait_ge(s_z[h % 3], 16 * loads * t + 16 * (h // 3 + 1))
                    dve.tensor_tensor(win, win, rel_win[:, h % 3, i, lo:W], ALU.add).then_inc(s_zadd, 1)
                    dve.wait_ge(s_zadd, NU * t + u + 1)
                    dve.tensor_reduce(negmax[:, c:c + 1], work[u % 2][:, 0:(i + 1) * P], AX.X, ALU.max,
                                      negate=True).then_inc(s_max, 1)
                if name == "ctx0":
                    dve.wait_ge(s_exp, NU * (t + 1))
                    dve.reciprocal(rdenom[:, :], denom[:, :]).then_inc(s_cn, 1)
                if name == "ctx4":
                    dve.wait_ge(s_cc, t + 1)
                    dve.wait_ge(s_crel, HG * (t + 1))
                    dve.tensor_tensor(ctx_s[:, :], ctx_s[:, :], work[1][:, :], ALU.add).then_inc(s_cn, 1)
                    dve.wait_ge(s_cn, 3 * t + 2)
                    heads = ctx_s[:, :].rearrange("p (c d) -> p c d", d=DH)
                    dve.tensor_tensor(heads, heads, rdenom[:, :, None].to_broadcast([P, NU, DH]),
                                      ALU.mult).then_inc(s_cn, 1)
                if name == "ctx5":
                    dve.wait_ge(s_chi, t + 1)
                    dve.tensor_tensor(ctx_t[:, LO, :], work[0][:, :], ctx_t[:, HI, :].bitcast(F32),
                                      ALU.subtract).then_inc(s_clo, 1)
                if name == "ctx6":
                    dve.wait_ge(s_o, t + 1)
                    dve.tensor_tensor(x2[:, :], work[1][:, :], x1[:, :], ALU.add).then_inc(s_x2, 1)

            def rotate(i, t):
                if i == 0:
                    wait(dve, s_pt, NU * t)
                    for b in range(2):
                        wait(dve, s_pst[b], 16 * (H // 2) * t)
                    if isinstance(t, int) and t == 0:
                        dve.wait_ge(s_wsplit_lo, E)
                a, b, bank_a, bank_b, scale = ((Q1, Q2, work[0], ctx_p, QSCALE), (K1, K2, work[1], work[0], 1.0))[i]
                dve.wait_ge(s_proj, 5 * t + 2 * i + 1)
                dve.scalar_tensor_tensor(out=a, in0=bank_a[:, :], scalar=scale, in1=cos_s[:, :],
                                         op0=ALU.mult, op1=ALU.mult).then_inc(s_rope, 1)
                dve.wait_ge(s_proj, 5 * t + 2 * i + 2)
                dve.scalar_tensor_tensor(out=b, in0=bank_b[:, :], scalar=scale, in1=sin_s[:, :],
                                         op0=ALU.mult, op1=ALU.mult).then_inc(s_rope, 1)
                dve.wait_ge(s_rope, 6 * t + 3 * i + 2)
                if i == 0:
                    dve.tensor_tensor(a, a, b, ALU.add).then_inc(s_rope, 1)
                else:
                    dve.scalar_tensor_tensor(out=a, in0=a, scalar=rel_k0[:, 0:1], in1=b,
                                             op0=ALU.add, op1=ALU.add).then_inc(s_rope, 1)

            whole_program(dve, chunk, flush, run, prologue, split_expert)

        @block.gpsimd
        def _(pool):
            def lo(n_pass, k):
                n = CH * n_pass + k
                pool.wait_ge(s_hhi, n + 1)
                pool.tensor_tensor(hid_lo[:, k % 2, :], hid[:, k % 2, :], hid_hi[:, k % 2, :].bitcast(F32),
                                   ALU.subtract).then_inc(s_hlo, 1)

            def chunk(n_pass, k, second, ln, led):
                if led >= 1:
                    lo(*before(n_pass, k, 1))

            def flush(n_pass):
                lo(n_pass, CH - 1)

            def split_expert(e):
                pool.wait_ge(s_wsplit_hi, e + 1)
                pool.tensor_tensor(wg[:, LO, e, :], stage[e % 2][:, 0:F], wg[:, HI, e, :].bitcast(F32), ALU.subtract)
                pool.tensor_tensor(wu[:, LO, e, :], stage[e % 2][:, F:2 * F], wu[:, HI, e, :].bitcast(F32),
                                   ALU.subtract).then_inc(s_wsplit_lo, 1)

            def prologue():
                pool.wait_ge(s_half, 1)
                norm(0)

            def norm(m):
                pool.wait_ge(s_mom, m + 1)
                pool.tensor_tensor(var_eps[:, :], moments[:, :, 1], eps[:, :], ALU.add).then_inc(s_ve, 1)
                pool.wait_ge(s_ve, m + 1)
                pool.tensor_tensor(rstd[:, :], var_eps[:, :], minus_half[:, :], ALU.pow).then_inc(s_rstd, 1)

            def run(name, arg, t):
                if name in ("ln1a", "ln2a", "ln3a"):
                    norm(ln_index(name, t))
                if name in ("proj2", "proj3"):
                    i = int(name[4]) - 2
                    pool.wait_ge(s_qkhi, 2 * t + i + 1)
                    pool.tensor_tensor(qk_r[:, 2 * i + 1, :], (Q1, K1)[i], qk[:, 2 * i, :],
                                       ALU.subtract).then_inc(s_qklo, 1)

            whole_program(pool, chunk, flush, run, prologue, split_expert)


_OUT = ((8, 512, 128), "float32")


def kernel(**inputs):
    import numpy as np
    import concourse.bacc as bacc
    from concourse import mybir
    from concourse.bass_utils import run_bass_kernel_spmd

    x = np.ascontiguousarray(inputs["L0_attn_x"])
    rel = np.asarray(inputs["L0_attn_rel_emb"])
    P, L, H, DH, R, HQ = 128, x.shape[1], 16, 8, 32, 4
    f32 = np.float32

    def dh_major(w):
        return np.asarray(w).reshape(H, DH, P).transpose(1, 0, 2)

    def swapped(w):
        return dh_major(w).reshape(DH // 2, 2, H, P)[:, ::-1].reshape(DH, H, P)

    order = np.array([HQ * (n % HQ) + n // HQ for n in range(H)])
    heads = np.asarray(inputs["L0_attn_w_v"]).reshape(H, DH, P)[order]
    w_o = np.asarray(inputs["L0_attn_w_o"]).reshape(P, H, DH)[:, order].reshape(P, P)
    watt = np.stack([m.reshape(P, P).T for m in (
        dh_major(inputs["L0_attn_w_q"]), swapped(inputs["L0_attn_w_q"]),
        dh_major(inputs["L0_attn_w_k"]), swapped(inputs["L0_attn_w_k"]), heads, w_o)], axis=1)

    rel_g, rel_g0 = np.zeros((HQ, 4, DH, HQ, R), rel.dtype), np.zeros((HQ, 4, DH, HQ, R), rel.dtype)
    rel_c, rel_c0 = np.zeros((HQ, R, HQ, DH), rel.dtype), np.zeros((HQ, R, HQ, DH), rel.dtype)
    for a in range(HQ):
        rel_g[a, :, :, a, :] = rel[1:R + 1].T
        rel_g0[a, :, :, a, :] = rel[0][:, None]
        rel_c[a, :, a, :] = rel[1:R + 1]
        rel_c0[a, :, a, :] = rel[0]

    inv_freq = 1.0 / 10000.0 ** (np.arange(0, DH, 2, dtype=f32) / DH)
    angle = np.outer(inv_freq.astype(f32), np.arange(L, dtype=f32)).astype(f32)
    cos = np.repeat(np.cos(angle.astype(np.float64)), 2, axis=0)
    sin = np.repeat(np.sin(angle.astype(np.float64)), 2, axis=0) * np.tile([-1.0, 1.0], DH // 2)[:, None]
    i, w = np.arange(P)[:, None], np.arange(P + R)[None, :]
    window = np.where(w > i + R, -1e30, 0.0)
    lanes = np.tile(np.repeat([[0.0, 1.0], [1.0, -1.0], [0.0, 1.0], [1.0, -1.0]], DH, axis=0), (HQ, 1))

    arrays = {
        "x": x, "wg": inputs["L0_ffn_Wg"], "wu": inputs["L0_ffn_Wu"], "wd": inputs["L0_ffn_Wd"],
        "watt": watt.reshape(P, -1), "rel_g": rel_g.reshape(P, P), "rel_g0": rel_g0.reshape(P, P),
        "rel_c": rel_c.reshape(P, R), "rel_c0": rel_c0.reshape(P, R),
        "rel_k0": np.repeat(rel[0], H)[:, None], "rel_v0": np.tile(rel[0], (P, H)),
        "cos": np.repeat(cos, H, axis=0).astype(f32), "sin": np.repeat(sin, H, axis=0).astype(f32),
        "window": window.astype(f32), "ident": np.eye(P, dtype=f32), "lanes": lanes.astype(f32),
    }
    nc = bacc.Bacc("TRN2", target_bir_lowering=False, num_devices=1)
    given, args = {}, []
    for name, a in arrays.items():
        a = np.ascontiguousarray(a)
        given[f"in_{name}"] = a
        args.append(nc.dram_tensor(f"in_{name}", a.shape, mybir.dt.from_np(a.dtype), kind="ExternalInput").ap())
    args.append(nc.dram_tensor("out", _OUT[0], mybir.dt.float32, kind="ExternalOutput").ap())
    macaron_kernel(nc, *args)
    return run_bass_kernel_spmd(nc, [given], core_ids=[0]).results[0]["out"]
```

```python
import concourse.bass as bass
from concourse import mybir
from contextlib import ExitStack


def macaron_kernel(nc, x_d, wg_d, wu_d, wd_d, watt_d, rel_g_d, rel_g0_d, rel_c_d, rel_c0_d,
                   rel_k0_d, rel_v0_d, cos_d, sin_d, window_d, ident_d, lanes_d, out_d):
    F32 = mybir.dt.float32
    F32R = mybir.dt.float32r
    F16 = mybir.dt.float16
    BF16 = mybir.dt.bfloat16
    ALU = mybir.AluOpType
    ACT = mybir.ActivationFunctionType
    AX = mybir.AxisListType

    P = 128
    B, L, D = x_d.shape
    E, _, F = wg_d.shape
    FC = F // P
    CH = E * FC
    NT = L // P
    H = 16
    DH = D // H
    R = 32
    HQ = 4
    HG = H // HQ
    W = P + R
    NU = H * NT
    QSCALE = float(DH) ** -0.5
    EPS = 1e-5
    LAG = 2
    TILE = P * W
    HI, LO = 0, 1
    VP = 3
    PSCALE = 2.0 ** 15
    GU = HQ * NT
    PROBS_16 = 3

    zwin_h = nc.dram_tensor("rel_window_scratch", [H * NT * TILE], F32, kind="Internal")
    pwin_h = nc.dram_tensor("prob_window_scratch", [H * NT * TILE], F32, kind="Internal")
    q_h = nc.dram_tensor("q_scratch", [4 * P * L], F32, kind="Internal")
    k_h = nc.dram_tensor("k_scratch", [4 * P * L], F32, kind="Internal")
    zwin_t, pwin_t, q_t, k_t = (h.ap().tensor for h in (zwin_h, pwin_h, q_h, k_h))

    ctx = ExitStack()
    with ctx:
        def sb(name, shape, dt=F32):
            return ctx.enter_context(nc.sbuf_tensor(name, shape, dt))

        def pb(name, shape):
            return ctx.enter_context(nc.psum_tensor(name, shape, F32))

        def sem(name):
            return ctx.enter_context(nc.semaphore(name))

        wg = sb("wg", [P, 2, E, F], F32R)
        wu = sb("wu", [P, 2, E, F], F32R)
        wd = sb("wd", [P, 2, E, F], F32R)
        watt = sb("watt", [P, 2, 6, P], F32R)
        WQ, WQS, WK, WKS, WV, WO = range(6)
        x0 = sb("x0", [P, L])
        x1 = sb("x1", [P, L])
        x2 = sb("x2", [P, L])
        xn = sb("xn", [P, L])
        xt1 = sb("xt1", [P, 2, L], F32R)
        xt2 = sb("xt2", [P, 2, L], F32R)
        acc_t = sb("acc_t", [P, L])
        out_s = xn
        th = sb("th", [P, 2, L])
        hid = sb("hid", [P, 2, L])
        hid_hi = sb("hid_hi", [P, 2, L], F32R)
        hid_lo = sb("hid_lo", [P, 2, L], F32R)
        cos_s = sb("cos_s", [P, L])
        sin_s = sb("sin_s", [P, L])
        qq = sb("qq", [P, HG, L], F32R)
        kk = sb("kk", [P, HG, L], F32R)
        v_s = acc_t
        v_b = sb("v_b", [P, VP, NT, P], BF16)
        rel_win = sb("rel_win", [P, 3, NT, W])
        g_a = sb("g_a", [P, NT, H, R])
        probs = sb("probs", [P, 2, R + NT * L])
        probs_16 = sb("probs_16", [P, PROBS_16, 2, L], F16)
        probs_t = sb("probs_t", [P, 2, 2, L], F16)
        band_t = sb("band_t", [P, L])
        ctx_s = sb("ctx_s", [P, L])
        ctx_t = xt2
        negmax = sb("negmax", [P, NU])
        denom = sb("denom", [P, NU])
        rdenom = sb("rdenom", [P, NU])
        rel_g = sb("rel_g", [P, P], F32R)
        rel_c = sb("rel_c", [P, R])
        rel_k0 = sb("rel_k0", [P, 1])
        rel_v0 = sb("rel_v0", [P, P])
        ident = sb("ident", [P, P])
        ident_16 = sb("ident_16", [P, P], F16)
        lanes = sb("lanes", [P, 2])
        stats = sb("stats", [P, NT, 6])
        moments = sb("moments", [P, NT, 2])
        var_eps = sb("var_eps", [P, NT])
        rstd = sb("rstd", [P, NT])
        minus_half = sb("minus_half", [P, NT])
        eps = sb("eps", [P, NT])
        settled = sb("settled", [P, 1])

        rope = [probs[:, 0, R + i * L:R + (i + 1) * L] for i in range(4)]
        Q1, Q2, K1, K2 = rope
        qk = probs[:, 1, R:].rearrange("p (c l) -> p c l", c=4)
        qk_r = qk.bitcast(F32R)
        stage = [probs[:, i, R:R + 3 * F] for i in range(2)]
        raw_att = g_a[:, :, :, :].rearrange("p a b c -> p (a b c)")[:, 0:6 * P]
        raw_rel = g_a[:, :, :, :].rearrange("p a b c -> p (a b c)")[:, 6 * P:6 * P + 2 * P + 2 * R]
        window = rel_win[:, 0, 0, :]
        v_rows = v_s[:, :].rearrange("p (a b) -> p a b", a=NT)

        gate = [pb(f"gate{i}", [P, L]) for i in range(2)]
        up = pb("up", [P, L])
        acc = pb("acc", [P, L])
        work = [pb(f"work{i}", [P, L]) for i in range(3)]
        ctx_p = pb("ctx_p", [P, L])
        turned = work[2][:, :].bitcast(F16).rearrange("p (a b) -> p a b", a=2)
        summed = ctx_p[:, 0:GU * VP * DH]

        s_w = [sem(f"expert_loaded{i}") for i in range(2)]
        s_wsplit_hi = sem("expert_hi")
        s_wsplit_lo = sem("expert_up_lo")
        s_wsplit_dlo = sem("expert_down_lo")
        s_const = sem("constants_loaded")
        s_win = sem("window_loaded")
        s_half = sem("exponent_set")
        s_pad = sem("pads_zeroed")
        s_att_hi = sem("att_weights_hi")
        s_att_lo = sem("att_weights_lo")
        s_rel = sem("rel_prepared")
        s_gate = sem("gate_ready")
        s_up = sem("up_ready")
        s_tanh = sem("tanh_ready")
        s_act = sem("gated_ready")
        s_hid = sem("hid_ready")
        s_hhi = sem("hid_hi_ready")
        s_hlo = sem("hid_lo_ready")
        s_down = sem("down_done")
        s_acc = sem("acc_copied")
        s_ftok = sem("ffn_tokens")
        s_sum = sem("residual_summed")
        s_st = sem("stats_done")
        s_mom = sem("moments_ready")
        s_ve = sem("var_eps_ready")
        s_rstd = sem("rstd_ready")
        s_xn = sem("xn_ready")
        s_xnt = sem("xn_transposed")
        s_xhi = sem("xt_hi_ready")
        s_xlo = sem("xt_lo_ready")
        s_vhi = sem("v_part_ready")
        s_id16 = sem("ident_16_ready")
        s_proj = sem("projected")
        s_rope = sem("rope_step")
        s_qkhi = sem("qk_hi_ready")
        s_qklo = sem("qk_lo_ready")
        s_v = sem("v_step")
        s_qkst = [sem(f"{x}_stored") for x in "qk"]
        s_qkld = sem("qk_loaded")
        s_g = sem("qrel_done")
        s_gev = sem("qrel_copied")
        s_gst = sem("qrel_stored")
        s_z = [sem(f"window_of_head_loaded{i}") for i in range(3)]
        s_sc = sem("scores_ready")
        s_zadd = sem("window_added")
        s_max = sem("max_ready")
        s_exp = sem("probs_ready")
        s_phi = sem("probs_hi_ready")
        s_plo = sem("probs_lo_ready")
        s_pt = sem("probs_transposed")
        s_ptc = sem("probs_t_copied")
        s_pv = sem("pv_done")
        s_pst = [sem(f"prob_window_stored{i}") for i in range(2)]
        s_band = sem("band_loaded")
        s_bt = sem("band_transposed")
        s_btc = sem("band_t_copied")
        s_crel = sem("ctx_rel_ready")
        s_cc = sem("ctx_of_group_summed")
        s_cn = sem("ctx_step")
        s_ct = sem("ctx_transposed")
        s_chi = sem("ctx_t_hi")
        s_clo = sem("ctx_t_lo")
        s_o = sem("attention_out")
        s_x2 = sem("attention_summed")
        s_x = sem("x_loaded")
        s_out = sem("dram_filled_then_outputs_stored")

        x_v = x_d.rearrange("b (t p) d -> b p t d", p=P)
        out_v = out_d.rearrange("b (t p) d -> b p t d", p=P)

        def column(h, i):
            return i * H + h

        def wait(eng, semaphore, value):
            if not (isinstance(value, int) and value <= 0):
                eng.wait_ge(semaphore, value)

        NORM2 = [("acc1", 0), ("sum1", 1), ("add1", 2), ("ln2a", 2), ("ln2b", 4), ("ln2t", 6), ("ln2h", 6),
                 ("ln2c", 7)]
        PROJECT = [("proj1", 0), ("rot1", 0), ("proj2", 2), ("qhi", 3), ("rot2", 3), ("proj3", 4), ("khi", 6),
                   ("vadd", 6), ("vsplit1", 8), ("vsplit2", 10)]
        NORM1 = [("ln1a", 0), ("ln1b", 2), ("ln1t", 4), ("ln1h", 4), ("ln1c", 5)]
        QREL = [("qrel1", 0), ("qrelcopy1", 1), ("qrel2", 2), ("qrelcopy2", 3)]
        CONTEXT = [("band0", 0), ("bandcopy0", 1), ("band1", 2), ("bandcopy1", 3), ("band2", 4), ("bandcopy2", 5),
                   ("band3", 6), ("bandcopy3", 7), ("band4", 8), ("scale", 9), ("ctxt", 12), ("ctxhi", 12),
                   ("ctxlo", 13), ("outproj", 15), ("attsum", 16), ("ln3a", 16), ("ln3b", 18), ("ln3t", 20),
                   ("ln3h", 20), ("ln3c", 21)]

        def plan(parts, ahead, lists, first, last, context_at, out_at):
            pieces = [[] for _ in range(parts + 1)]

            def put(names, at):
                for name, after in names:
                    pieces[min(at + after, parts)].append((name, 0))

            for names, at in lists:
                put(names, at)
            halves = 2 * (NU + 4)
            for n in range(halves):
                pieces[first + n * (last - first) // halves].append((("score", "turn")[n % 2], n // 2))
            if out_at == parts:
                pieces[parts] += [("acc2", 0), ("sum2", NU + 1), ("add2", 0)]
            elif out_at is not None:
                pieces[out_at].append(("acc2", 0))
                for slot in pieces[out_at + 2:]:
                    units = [i for i, (name, u) in enumerate(slot) if name == "score" and u % 2 == 0]
                    if units:
                        u = slot[units[0]][1]
                        slot[units[0]:units[0] + 1] = [("sum2", u), ("add2", 0), ("score_after_sum2", u)]
                        break
            put(CONTEXT, context_at)
            return [(name, 0) for names in ahead for name, _ in names], pieces

        START = 3 * LAG - 1
        FULL = 2 * 3 * CH
        FULL_STEP = plan(FULL, [], [(NORM2, START), (PROJECT, START + 9), (NORM1, START + 18), (QREL, START + 34)],
                         START + 42, FULL - 22, FULL - 21, FULL // 2 + START)
        FIRST_STEP = plan(3 * CH, [NORM2, PROJECT, NORM1, QREL], [], 6, 3 * CH, 3 * CH, None)
        LAST_STEP = plan(3 * CH, [], [(NORM2, START), (PROJECT, START + 9), (QREL, START + 28)],
                         START + 36, 3 * CH, 3 * CH, 3 * CH)

        def ln_index(name, t):
            after_ln2 = 1 if not isinstance(t, int) or t < B - 1 else 0
            return 3 * t + 1 + {"ln2": 0, "ln1": 1, "ln3": 1 + after_ln2}[name[:3]]

        def sum_index(name, t):
            first = 2 * t - 1 if not isinstance(t, int) or t > 0 else 0
            return {"1": first, "2": 2 * t, "t": 2 * B - 1}[name[-1]]

        def before(n_pass, k, j):
            return (n_pass, k - j) if k >= j else (n_pass - 1, CH + k - j)

        def whole_program(eng, chunk, flush, run, prologue, split_expert):
            def passes(t, order, pieces):
                for m, (n_pass, second, ln, led) in enumerate(order):
                    for k in range(CH):
                        for part in range(3):
                            chunk(part, n_pass, k, second, ln, min(led + k, CH))
                            for name, arg in pieces[3 * (CH * m + k) + part]:
                                run(name, arg, t)

            prologue()
            split_expert(0)
            for k in range(CH):
                for part in range(3):
                    chunk(part, 0, k, False, 0, k)
                if k % FC == 0 and k // FC + 1 < E:
                    split_expert(k // FC + 1)
            flush(0)
            ahead, pieces = FIRST_STEP
            for name, arg in ahead:
                run(name, arg, 0)
            passes(0, [(1, False, ln_index("ln1", 0), 0)], pieces)
            for name, arg in pieces[3 * CH]:
                run(name, arg, 0)
            with eng.Fori(1, B - 1) as t:
                ahead, pieces = FULL_STEP
                passes(t, [(2 * t, True, 3 * t, CH), (2 * t + 1, False, ln_index("ln1", t), CH)], pieces)
                for name, arg in pieces[2 * 3 * CH]:
                    run(name, arg, t)
            t = B - 1
            ahead, pieces = LAST_STEP
            passes(t, [(2 * t, True, 3 * t, CH)], pieces)
            flush(2 * t)
            for name, arg in pieces[3 * CH]:
                run(name, arg, t)
            for k in range(CH):
                for part in range(3):
                    chunk(part, 2 * B - 1, k, True, ln_index("ln3", t), k)
            flush(2 * B - 1)
            for name in ("acclast", "sumlast", "addlast"):
                run(name, 0, B)

        block = ctx.enter_context(nc.Block())

        @block.sync
        def _(sp):
            def no_chunk(part, n_pass, k, second, ln, led):
                pass

            def no_split(e):
                pass

            def no_flush(n_pass):
                pass

            def prologue():
                sp.dma_start(x0[:, :].rearrange("p (t d) -> p t d", t=NT), x_v[0]).then_inc(s_x, 16)
                for i, (dst, src) in enumerate(((ident[:, :], ident_d), (window, window_d),
                                                (raw_att, watt_d), (cos_s[:, :], cos_d),
                                                (sin_s[:, :], sin_d), (rel_k0[:, :], rel_k0_d),
                                                (rel_v0[:, :], rel_v0_d), (lanes[:, :], lanes_d),
                                                (raw_rel[:, 0:P], rel_g_d), (raw_rel[:, P:2 * P], rel_g0_d),
                                                (raw_rel[:, 2 * P:2 * P + R], rel_c_d),
                                                (raw_rel[:, 2 * P + R:], rel_c0_d))):
                    if i == 2:
                        for e in range(2):
                            load_expert(e)
                    sp.dma_start(dst, src).then_inc(s_win if i == 1 else s_const, 16)
                for e in range(2, E):
                    sp.wait_ge(s_wsplit_hi, e - 1)
                    sp.wait_ge(s_wsplit_lo, e - 1)
                    sp.wait_ge(s_wsplit_dlo, e - 1)
                    load_expert(e)
                sp.wait_ge(s_win, 16)
                sp.dma_start(bass.AP(zwin_t, 0, [[W, P], [TILE, H * NT], [1, W]]),
                             window[:, None, :].to_broadcast([P, H * NT, W])).then_inc(s_out, 16)
                sp.wait_ge(s_out, 16)

            def load_expert(e):
                dst = stage[e % 2]
                sp.dma_start(dst[:, 0:F], wg_d[e]).then_inc(s_w[e % 2], 16)
                sp.dma_start(dst[:, F:2 * F], wu_d[e]).then_inc(s_w[e % 2], 16)
                sp.dma_start(dst[:, 2 * F:3 * F].rearrange("p (c d) -> p c d", c=FC),
                             wd_d[e].rearrange("(c p) d -> p c d", p=P)).then_inc(s_w[e % 2], 16)

            def load_window(h, t):
                if h >= 3:
                    sp.wait_ge(s_zadd, NU * t + NT * (h - 2))
                sp.dma_start(rel_win[:, h % 3, :, :],
                             bass.AP(zwin_t, h * NT * TILE, [[W, P], [TILE, NT], [1, W]])).then_inc(s_z[h % 3], 16)

            def run(name, arg, t):
                if name == "add1" and (not isinstance(t, int) or t < B - 1):
                    sp.wait_ge(s_sum, sum_index("sum1", t) + 1)
                    sp.dma_start(x0[:, :].rearrange("p (t d) -> p t d", t=NT),
                                 x_v[t + 1]).then_inc(s_x, 16)
                if name in ("qhi", "khi"):
                    k = int(name == "khi")
                    scratch, dst = ((q_t, qq), (k_t, kk))[k]
                    sp.wait_ge(s_qkhi, 2 * t + 1 + k)
                    sp.wait_ge(s_qklo, 2 * t + 1 + k)
                    for copy in range(2):
                        sp.dma_start(bass.AP(scratch, copy * (1 + k) * P * L, [[L, P], [(2 - k) * P * L, 2], [1, L]]),
                                     qk[:, 2 * k:2 * k + 2, :]).then_inc(s_qkst[k], 16)
                    sp.wait_ge(s_qkst[k], 32 * (t + 1))
                    sp.dma_start(dst[:, :, :].bitcast(F32).rearrange("p g l -> p (g l)"),
                                 bass.AP(scratch, 0, [[HG * L, HQ], [H * L, 4 * DH], [1, HG * L]])
                                 ).then_inc(s_qkld, 16)
                if name == "qrel2":
                    for i in range(NT):
                        sp.wait_ge(s_gev, NT * t + i + 1)
                        sp.dma_start(bass.AP(zwin_t, i * TILE + 1, [[W + 1, P], [NT * TILE, H], [1, R]]),
                                     g_a[:, i, :, :]).then_inc(s_gst, 16)
                    sp.wait_ge(s_gst, 16 * NT * (t + 1))
                    for h in range(2):
                        load_window(h, t)
                if name[:5] == "score" and arg % NT == 0 and arg // NT + 2 < H:
                    load_window(arg // NT + 2, t)
                if name[:5] == "score" and arg >= NT and arg % NT == 1:
                    h = arg // NT - 1
                    if h < H:
                        sp.wait_ge(s_exp, NU * t + NT * (h + 1))
                        sp.dma_start(bass.AP(pwin_t, h * NT * TILE, [[W, P], [TILE, NT], [1, W]]),
                                     bass.AP(probs[:, h % 2, :].tensor, probs[:, h % 2, :].offset,
                                             [list(probs[:, h % 2, :].ap[0]), [L + P, NT], [1, W]])
                                     ).then_inc(s_pst[h % 2], 16)
                        sp.wait_ge(s_pst[h % 2], 16 * (H // 2) * t + 16 * (h // 2 + 1))
                        sp.dma_start(g_a[:, :, h, :],
                                     bass.AP(pwin_t, h * NT * TILE + 1, [[W + 1, P], [TILE, NT], [1, R]])
                                     ).then_inc(s_band, 16)
                if name == "add2":
                    sp.wait_ge(s_sum, sum_index("sum2", t) + 1)
                    sp.dma_start(out_v[t - 1], out_s[:, :].rearrange("p (t d) -> p t d", t=NT)).then_inc(s_out, 16)
                if name == "addlast":
                    sp.wait_ge(s_sum, 2 * B)
                    sp.dma_start(out_v[B - 1], out_s[:, :].rearrange("p (t d) -> p t d", t=NT)).then_inc(s_out, 16)
                    sp.wait_ge(s_out, 16 * (B + 1))

            whole_program(sp, no_chunk, no_flush, run, prologue, no_split)

        @block.tensor
        def _(pe):
            def three(out, w_hi, w_lo, m_hi, m_lo, start=True, stop=True):
                pe.matmul(out, w_hi, m_hi, start=start, stop=False)
                pe.matmul(out, w_hi, m_lo, start=False, stop=False)
                return pe.matmul(out, w_lo, m_hi, start=False, stop=stop)

            def transposes(dst, src, n=NT):
                for i in range(n):
                    last = pe.transpose(dst[:, i * P:(i + 1) * P], src[:, i * P:(i + 1) * P], ident[:, :])
                return last

            def down(n_pass, k):
                n = CH * n_pass + k
                e, c = k // FC, k % FC
                pe.wait_ge(s_hhi, n + 1)
                pe.wait_ge(s_hlo, n + 1)
                if k == 0:
                    wait(pe, s_acc, n_pass)
                three(acc[:, :], wd[:, HI, e, c * P:(c + 1) * P], wd[:, LO, e, c * P:(c + 1) * P],
                      hid_hi[:, k % 2, :], hid_lo[:, k % 2, :],
                      start=(k == 0), stop=(k == CH - 1)).then_inc(s_down, 1)

            def chunk(part, n_pass, k, second, ln, led):
                n = CH * n_pass + k
                e, c = k // FC, k % FC
                xt = xt2 if second else xt1
                if part == 1:
                    wait(pe, s_hid, n)
                    three(up[:, :], wu[:, HI, e, c * P:(c + 1) * P], wu[:, LO, e, c * P:(c + 1) * P],
                          xt[:, HI, :], xt[:, LO, :]).then_inc(s_up, 1)
                if part == 2 and led >= LAG:
                    down(*before(n_pass, k, LAG))
                if part > 0:
                    return
                if isinstance(n_pass, int) and n_pass == 0 and k % FC == 0:
                    pe.wait_ge(s_wsplit_hi, e + 1)
                    pe.wait_ge(s_wsplit_lo, e + 1)
                    pe.wait_ge(s_wsplit_dlo, e + 1)
                if k == 0:
                    pe.wait_ge(s_xhi, ln + 1)
                    pe.wait_ge(s_xlo, ln + 1)
                wait(pe, s_act, n - 1)
                three(gate[k % 2][:, :], wg[:, HI, e, c * P:(c + 1) * P], wg[:, LO, e, c * P:(c + 1) * P],
                      xt[:, HI, :], xt[:, LO, :]).then_inc(s_gate, 1)

            def flush(n_pass):
                for k in range(CH - LAG, CH):
                    down(n_pass, k)

            def prologue():
                pe.wait_ge(s_const, 16 * 11)
                pe.wait_ge(s_xn, 1)
                transposes(work[1], xn).then_inc(s_xnt, 1)

            def no_split(e):
                pass

            def run(name, arg, t):
                if name[:3] == "sum":
                    j = 2 * B - 1 if name == "sumlast" else sum_index(name, t)
                    pe.wait_ge(s_acc, j + 1)
                    if name == "sum2":
                        pe.wait_ge(s_exp, NU * t + arg - 1)
                    transposes(work[0], acc_t).then_inc(s_ftok, 1)
                if name in ("ln1t", "ln2t", "ln3t"):
                    pe.wait_ge(s_xn, ln_index(name, t) + 1)
                    transposes(work[1], xn).then_inc(s_xnt, 1)
                if name == "proj1":
                    if isinstance(t, int) and t == 0:
                        pe.wait_ge(s_id16, 1)
                        pe.wait_ge(s_att_hi, 1)
                        pe.wait_ge(s_att_lo, 1)
                    pe.wait_ge(s_xhi, ln_index("ln2", t) + 1)
                    pe.wait_ge(s_xlo, ln_index("ln2", t) + 1)
                    for w, bank in ((WQ, work[0]), (WQS, ctx_p)):
                        three(bank[:, :], watt[:, HI, w, :], watt[:, LO, w, :],
                              xt1[:, HI, :], xt1[:, LO, :]).then_inc(s_proj, 1)
                if name == "proj2":
                    three(work[1][:, :], watt[:, HI, WK, :], watt[:, LO, WK, :],
                          xt1[:, HI, :], xt1[:, LO, :]).then_inc(s_proj, 1)
                    three(work[2][:, :], watt[:, HI, WKS, :], watt[:, LO, WKS, :],
                          xt1[:, HI, :], xt1[:, LO, :]).then_inc(s_proj, 1)
                if name == "proj3":
                    pe.wait_ge(s_rope, 6 * t + 2)
                    for i in range(NT):
                        cols = slice(i * P, (i + 1) * P)
                        last = three(ctx_p[:, cols], xt1[:, HI, cols], xt1[:, LO, cols],
                                     watt[:, HI, WV, :], watt[:, LO, WV, :])
                    last.then_inc(s_proj, 1)
                if name == "qrel1":
                    pe.wait_ge(s_qkld, 32 * (t + 1))
                    pe.wait_ge(s_rope, 6 * t + 5)
                    if isinstance(t, int) and t == 0:
                        pe.wait_ge(s_rel, 3)
                    pe.wait_ge(s_v, VP * t + 1)
                if name in ("qrel1", "qrel2"):
                    for i in range(2):
                        bank = (work[0], ctx_p)[i]
                        tile = i + 2 * (name == "qrel2")
                        if name == "qrel2":
                            pe.wait_ge(s_gev, NT * t + i + 1)
                        for g in range(HG):
                            last = pe.matmul(bank[:, g * P:(g + 1) * P], qq[:, g, tile * P:(tile + 1) * P],
                                             rel_g[:, :], start=True, stop=True)
                        last.then_inc(s_g, 1)
                if name[:5] == "score":
                    if name == "score_after_sum2":
                        pe.wait_ge(s_sum, sum_index("sum2", t) + 1)
                    score(arg, t)
                if name[:4] == "band" and name[4:].isdigit():
                    context(int(name[4:]), t)
                if name == "ctxt":
                    context(5, t)
                if name == "outproj":
                    context(6, t)

            def score(n, t):
                if n < NU:
                    h, i = n // NT, n % NT
                    a, g = h % HQ, h // HQ
                    rows = slice(32 * a, 32 * a + 32)
                    if n == 0:
                        pe.wait_ge(s_gev, NT * t + NT)
                    if n == 1:
                        last_ln = "ln1" if not isinstance(t, int) or t < B - 1 else "ln2"
                        pe.wait_ge(s_xlo, ln_index(last_ln, t) + 1)
                    if n >= 2:
                        pe.wait_ge(s_exp, NU * t + n - 1)
                    cols = (i + 1) * P
                    pe.matmul(work[n % 2][:, 0:cols], qq[rows, g, i * P:(i + 1) * P], kk[rows, g, 0:cols],
                              start=True, stop=True).then_inc(s_sc, 1)
                if n >= 4:
                    u = n - 4
                    h, i = u // NT, u % NT
                    pe.wait_ge(s_ptc, NU * t + u + 1)
                    if u == 0:
                        pe.wait_ge(s_v, VP * t + VP)
                        pe.wait_ge(s_vhi, 2 * t + 2)
                    elif u % GU == 0:
                        pe.wait_ge(s_cc, HG * t + u // GU)
                    o = (i * HQ + h % HQ) * VP * DH
                    for j in range(i + 1):
                        for part in (HI, LO):
                            last = pe.matmul(ctx_p[:, o:o + VP * DH], probs_t[:, u % 2, part, j * P:(j + 1) * P],
                                             v_b[:, :, j, h * DH:(h + 1) * DH],
                                             start=(j == 0 and part == HI), stop=(j == i and part == LO))
                    last.then_inc(s_pv, 1)
                if 3 <= n < NU + 3:
                    u = n - 3
                    pe.wait_ge(s_plo, NU * t + u + 1)
                    if u >= 1:
                        pe.wait_ge(s_ptc, NU * t + u)
                    for part in (HI, LO):
                        for j in range(u % NT + 1):
                            last = pe.transpose(turned[:, part, j * P:(j + 1) * P],
                                                probs_16[:, u % PROBS_16, part, j * P:(j + 1) * P], ident_16[:, :])
                    last.then_inc(s_pt, 1)

            def context(step, t):
                if 1 <= step <= HG:
                    g = step - 1
                    pe.wait_ge(s_btc, HG * t + g + 1)
                    for i in range(NT):
                        o = i * P + g * HQ * DH
                        last = pe.matmul(work[1][:, o:o + HQ * DH], band_t[:, i * P:(i + 1) * P],
                                         rel_c[:, :], start=True, stop=True)
                    last.then_inc(s_crel, 1)
                if step < HG:
                    g = step
                    if g == 0:
                        pe.wait_ge(s_band, 16 * H * (t + 1))
                        pe.wait_ge(s_exp, NU * (t + 1))
                        if isinstance(t, int) and t == B - 1:
                            pe.wait_ge(s_sum, sum_index("sum2", t) + 1)
                    for i in range(NT):
                        last = pe.transpose(work[0][:, i * P:(i + 1) * P],
                                            g_a[:, i, g * HQ:(g + 1) * HQ, :].rearrange("p h r -> p (h r)"),
                                            ident[:, :])
                    last.then_inc(s_bt, 1)
                if step == 5:
                    pe.wait_ge(s_cn, 3 * t + 3)
                    transposes(work[0], ctx_s).then_inc(s_ct, 1)
                if step == 6:
                    pe.wait_ge(s_chi, t + 1)
                    pe.wait_ge(s_clo, t + 1)
                    for i in range(NT):
                        cols = slice(i * P, (i + 1) * P)
                        last = three(work[1][:, cols], ctx_t[:, HI, cols], ctx_t[:, LO, cols],
                                     watt[:, HI, WO, :], watt[:, LO, WO, :])
                    last.then_inc(s_o, 1)

            whole_program(pe, chunk, flush, run, prologue, no_split)

        @block.scalar
        def _(act):
            def hi(n_pass, k):
                n = CH * n_pass + k
                act.wait_ge(s_hid, n + 1)
                wait(act, s_down, n - 1)
                act.copy(hid_hi[:, k % 2, :], hid[:, k % 2, :]).then_inc(s_hhi, 1)

            def chunk(part, n_pass, k, second, ln, led):
                n = CH * n_pass + k
                if part == 0:
                    act.wait_ge(s_gate, n + 1)
                    wait(act, s_act, n - 1)
                    act.activation(th[:, k % 2, :], gate[k % 2][:, :], ACT.Tanh, scale=0.5).then_inc(s_tanh, 1)
                if part == 1 and led >= 1:
                    hi(*before(n_pass, k, 1))

            def flush(n_pass):
                hi(n_pass, CH - 1)

            def split_expert(e):
                act.wait_ge(s_w[e % 2], 48 * (e // 2 + 1))
                act.copy(wg[:, HI, e, :], stage[e % 2][:, 0:F])
                act.copy(wu[:, HI, e, :], stage[e % 2][:, F:2 * F])
                act.copy(wd[:, HI, e, :], stage[e % 2][:, 2 * F:3 * F]).then_inc(s_wsplit_hi, 1)

            def prologue():
                act.wait_ge(s_xnt, 1)
                act.copy(xt1[:, HI, :], work[1][:, :]).then_inc(s_xhi, 1)
                act.wait_ge(s_const, 16 * 11)
                act.copy(ident_16[:, :], ident[:, :]).then_inc(s_id16, 1)
                act.copy(watt[:, HI, :, :].rearrange("p a b -> p (a b)"), raw_att).then_inc(s_att_hi, 1)

            def run(name, arg, t):
                if name[:3] == "acc":
                    j = 2 * B - 1 if name == "acclast" else sum_index(name, t)
                    act.wait_ge(s_down, CH * (j + 1))
                    wait(act, s_ftok, j)
                    act.mul(acc_t[:, :], acc[:, :], 0.25).then_inc(s_acc, 1)
                if name in ("ln1h", "ln2h", "ln3h"):
                    xt = xt2 if name == "ln3h" else xt1
                    act.wait_ge(s_xnt, ln_index(name, t) + 1)
                    act.copy(xt[:, HI, :], work[1][:, :]).then_inc(s_xhi, 1)
                if name in ("qhi", "khi"):
                    i = int(name == "khi")
                    act.wait_ge(s_rope, 6 * t + 3 * (i + 1))
                    act.copy(qk_r[:, 2 * i, :], (Q1, K1)[i]).then_inc(s_qkhi, 1)
                if name in ("qrelcopy1", "qrelcopy2"):
                    for i in range(2):
                        tile = i + 2 * (name == "qrelcopy2")
                        act.wait_ge(s_g, NT * t + tile + 1)
                        act.copy(g_a[:, tile, :, :].rearrange("p h r -> p (h r)"),
                                 (work[0], ctx_p)[i][:, :]).then_inc(s_gev, 1)
                if name[:5] == "score" and 1 <= arg <= NU:
                    exponentials(arg - 1, t)
                if name == "turn" and 3 <= arg < NU + 3:
                    u = arg - 3
                    cols = (u % NT + 1) * P
                    act.wait_ge(s_pt, NU * t + u + 1)
                    if u >= 2:
                        act.wait_ge(s_pv, NU * t + u - 1)
                    act.mul(probs_t[:, u % 2, :, 0:cols], turned[:, :, 0:cols], PSCALE).then_inc(s_ptc, 1)
                if name in ("vsplit1", "vsplit2"):
                    n = int(name[6]) - 1
                    act.wait_ge(s_v, VP * t + n + 1)
                    act.copy(v_b[:, n, :, :], v_rows).then_inc(s_vhi, 1)
                if name[:8] == "bandcopy":
                    g = int(name[8:])
                    act.wait_ge(s_bt, HG * t + g + 1)
                    if g > 0:
                        act.wait_ge(s_crel, HG * t + g)
                    act.copy(band_t[:, :], work[0][:, :]).then_inc(s_btc, 1)
                if name == "ctxhi":
                    act.wait_ge(s_ct, t + 1)
                    act.copy(ctx_t[:, HI, :], work[0][:, :]).then_inc(s_chi, 1)

            def exponentials(u, t):
                h, i = u // NT, u % NT
                act.wait_ge(s_max, NU * t + u + 1)
                if i == 0 and h >= 2:
                    act.wait_ge(s_pst[h % 2], 16 * (H // 2) * t + 16 * (h // 2))
                if u == 0:
                    act.wait_ge(s_qkst[0], 32 * (t + 1))
                    act.wait_ge(s_qkst[1], 32 * (t + 1))
                c = column(h, i)
                act.activation(probs[:, h % 2, R + i * L:R + i * L + (i + 1) * P],
                               work[u % 2][:, 0:(i + 1) * P], ACT.Exp,
                               bias=negmax[:, c:c + 1], accum_out=denom[:, c:c + 1]).then_inc(s_exp, 1)

            whole_program(act, chunk, flush, run, prologue, split_expert)

        @block.vector
        def _(dve):
            def chunk(part, n_pass, k, second, ln, led):
                n = CH * n_pass + k
                if part == 1:
                    dve.wait_ge(s_act, n + 1)
                    dve.wait_ge(s_up, n + 1)
                    dve.tensor_tensor(hid[:, k % 2, :], hid[:, k % 2, :], up[:, :],
                                      ALU.mult).then_inc(s_hid, 1)
                if part > 0:
                    return
                dve.wait_ge(s_tanh, n + 1)
                wait(dve, s_hlo, n - 1)
                dve.scalar_tensor_tensor(out=hid[:, k % 2, :], in0=th[:, k % 2, :], scalar=1.0,
                                         in1=gate[k % 2][:, :], op0=ALU.add, op1=ALU.mult).then_inc(s_act, 1)

            def flush(n_pass):
                pass

            def split_expert(e):
                dve.wait_ge(s_wsplit_hi, e + 1)
                dve.tensor_tensor(wd[:, LO, e, :], stage[e % 2][:, 2 * F:3 * F],
                                  wd[:, HI, e, :].bitcast(F32), ALU.subtract).then_inc(s_wsplit_dlo, 1)

            def prologue():
                dve.memset(minus_half[:, :], -0.5)
                dve.memset(eps[:, :], EPS).then_inc(s_half, 1)
                dve.memset(probs[:, :, 0:R], 0.0).then_inc(s_pad, 1)
                dve.wait_ge(s_x, 16)
                norm_a(0, x0)
                norm_b(0, x0)
                norm_c(0, xt1)
                dve.wait_ge(s_const, 16 * 11)
                dve.wait_ge(s_att_hi, 1)
                dve.tensor_tensor(watt[:, LO, :, :].rearrange("p a b -> p (a b)"), raw_att,
                                  watt[:, HI, :, :].rearrange("p a b -> p (a b)").bitcast(F32),
                                  ALU.subtract).then_inc(s_att_lo, 1)
                dve.tensor_tensor(rel_c[:, :], raw_rel[:, 2 * P:2 * P + R], raw_rel[:, 2 * P + R:],
                                  ALU.subtract)
                dve.tensor_tensor(raw_rel[:, 0:P], raw_rel[:, 0:P], raw_rel[:, P:2 * P],
                                  ALU.subtract).then_inc(s_rel, 1)
                dve.wait_ge(s_rel, 1)
                dve.tensor_copy(ctx_s[:, 0:P].bitcast(F32R), raw_rel[:, 0:P])
                dve.tensor_scalar(raw_rel[:, P:2 * P], raw_rel[:, 0:P], lanes[:, 0:1], None,
                                  ALU.mult).then_inc(s_rel, 1)
                dve.wait_ge(s_rel, 2)
                dve.scalar_tensor_tensor(out=rel_g[:, :], in0=ctx_s[:, 0:P], scalar=lanes[:, 1:2],
                                         in1=raw_rel[:, P:2 * P], op0=ALU.mult, op1=ALU.add).then_inc(s_rel, 1)

            def norm_a(m, x):
                for i in range(NT):
                    last = dve.bn_stats(stats[:, i, :], x[:, i * P:(i + 1) * P])
                last.then_inc(s_st, 1)
                dve.wait_ge(s_st, m + 1)
                dve.memset(settled[:, :], 0.0)
                for i in range(NT):
                    last = dve.bn_aggr(moments[:, i, :], stats[:, i, :])
                last.then_inc(s_mom, 1)

            def norm_b(m, x, t=None):
                if x is x2:
                    dve.wait_ge(s_out, 16 * (t + 1))
                dve.wait_ge(s_rstd, m + 1)
                wait(dve, s_xnt, m)
                for i in range(NT):
                    last = dve.tensor_scalar(xn[:, i * P:(i + 1) * P], x[:, i * P:(i + 1) * P],
                                             moments[:, i, 0:1], rstd[:, i:i + 1], ALU.subtract, ALU.mult)
                last.then_inc(s_xn, 1)

            def norm_c(m, xt):
                dve.wait_ge(s_xhi, m + 1)
                dve.tensor_tensor(xt[:, LO, :], work[1][:, :], xt[:, HI, :].bitcast(F32),
                                  ALU.subtract).then_inc(s_xlo, 1)

            def run(name, arg, t):
                if name == "add1":
                    dve.wait_ge(s_ftok, sum_index(name, t) + 1)
                    dve.wait_ge(s_x, 16 * (t + 1))
                    dve.tensor_tensor(x1[:, :], work[0][:, :], x0[:, :], ALU.add).then_inc(s_sum, 1)
                if name in ("add2", "addlast"):
                    j = 2 * B - 1 if name == "addlast" else sum_index(name, t)
                    dve.wait_ge(s_ftok, j + 1)
                    dve.wait_ge(s_out, 16 * t)
                    dve.tensor_tensor(out_s[:, :], work[0][:, :], x2[:, :], ALU.add).then_inc(s_sum, 1)
                if name == "ln2a":
                    dve.wait_ge(s_sum, sum_index("sum1", t) + 1)
                if name == "ln3a":
                    dve.wait_ge(s_x2, t + 1)
                if name == "ln1a":
                    dve.wait_ge(s_x, 16 * (t + 2))
                if name[:2] == "ln":
                    m = ln_index(name, t)
                    x = {"1": x0, "2": x1, "3": x2}[name[2]]
                    if name[3] == "a":
                        norm_a(m, x)
                    if name[3] == "b":
                        norm_b(m, x, t)
                    if name[3] == "c":
                        norm_c(m, xt2 if name[2] == "3" else xt1)
                if name in ("rot1", "rot2"):
                    rotate(int(name[3]) - 1, t)
                if name == "vadd":
                    dve.wait_ge(s_proj, 5 * t + 5)
                    dve.tensor_tensor(v_rows, ctx_p[:, :].rearrange("p (a b) -> p a b", a=NT),
                                      rel_v0[:, None, :].to_broadcast([P, NT, P]), ALU.add).then_inc(s_v, 1)
                if name[:5] == "score" and arg < NU:
                    u, h, i = arg, arg // NT, arg % NT
                    c = column(h, i)
                    lo = R if i == 0 else 0
                    win = work[u % 2][:, i * P - R + lo:(i + 1) * P]
                    dve.wait_ge(s_sc, NU * t + u + 1)
                    if i == 0:
                        loads = len(range(h % 3, H, 3))
                        dve.wait_ge(s_z[h % 3], 16 * loads * t + 16 * (h // 3 + 1))
                    dve.tensor_tensor(win, win, rel_win[:, h % 3, i, lo:W], ALU.add).then_inc(s_zadd, 1)
                    dve.wait_ge(s_zadd, NU * t + u + 1)
                    dve.tensor_reduce(negmax[:, c:c + 1], work[u % 2][:, 0:(i + 1) * P], AX.X, ALU.max,
                                      negate=True).then_inc(s_max, 1)
                if name == "turn" and 1 <= arg <= NU:
                    u = arg - 1
                    h, i = u // NT, u % NT
                    dve.wait_ge(s_exp, NU * t + u + 1)
                    if u >= PROBS_16:
                        dve.wait_ge(s_pt, NU * t + u + 1 - PROBS_16)
                    dve.tensor_copy(probs_16[:, u % PROBS_16, HI, 0:(i + 1) * P],
                                    probs[:, h % 2, R + i * L:R + i * L + (i + 1) * P]).then_inc(s_phi, 1)
                if name == "turn" and arg >= GU + 3 and (arg - 3) % GU == 0:
                    g = (arg - 3) // GU - 1
                    dve.wait_ge(s_pv, NU * t + GU * (g + 1))
                    dve.tensor_reduce(ctx_s[:, :].rearrange("p (i g a d) -> p g i a d", i=NT, g=HG, d=DH)[:, g],
                                      summed.rearrange("p (i a s d) -> p i a d s", i=NT, s=VP, d=DH), AX.X,
                                      ALU.add).then_inc(s_cc, 1)
                if name == "band1":
                    dve.wait_ge(s_exp, NU * (t + 1))
                    dve.reciprocal(rdenom[:, :], denom[:, :]).then_inc(s_cn, 1)
                if name == "scale":
                    dve.wait_ge(s_cc, HG * (t + 1))
                    dve.wait_ge(s_crel, HG * (t + 1))
                    dve.scalar_tensor_tensor(out=ctx_s[:, :], in0=ctx_s[:, :], scalar=1.0 / PSCALE,
                                             in1=work[1][:, :], op0=ALU.mult, op1=ALU.add).then_inc(s_cn, 1)
                    dve.wait_ge(s_cn, 3 * t + 2)
                    heads = ctx_s[:, :].rearrange("p (c d) -> p c d", d=DH)
                    dve.tensor_tensor(heads, heads, rdenom[:, :, None].to_broadcast([P, NU, DH]),
                                      ALU.mult).then_inc(s_cn, 1)
                if name == "ctxlo":
                    dve.wait_ge(s_chi, t + 1)
                    dve.tensor_tensor(ctx_t[:, LO, :], work[0][:, :], ctx_t[:, HI, :].bitcast(F32),
                                      ALU.subtract).then_inc(s_clo, 1)
                if name == "attsum":
                    dve.wait_ge(s_o, t + 1)
                    dve.tensor_tensor(x2[:, :], work[1][:, :], x1[:, :], ALU.add).then_inc(s_x2, 1)

            def rotate(i, t):
                if i == 0:
                    wait(dve, s_pt, NU * t)
                    for b in range(2):
                        wait(dve, s_pst[b], 16 * (H // 2) * t)
                    if isinstance(t, int) and t == 0:
                        dve.wait_ge(s_wsplit_lo, E)
                a, b, bank_a, bank_b, scale = ((Q1, Q2, work[0], ctx_p, QSCALE), (K1, K2, work[1], work[2], 1.0))[i]
                dve.wait_ge(s_proj, 5 * t + 2 * i + 1)
                dve.scalar_tensor_tensor(out=a, in0=bank_a[:, :], scalar=scale, in1=cos_s[:, :],
                                         op0=ALU.mult, op1=ALU.mult).then_inc(s_rope, 1)
                dve.wait_ge(s_proj, 5 * t + 2 * i + 2)
                dve.scalar_tensor_tensor(out=b, in0=bank_b[:, :], scalar=scale, in1=sin_s[:, :],
                                         op0=ALU.mult, op1=ALU.mult).then_inc(s_rope, 1)
                dve.wait_ge(s_rope, 6 * t + 3 * i + 2)
                if i == 0:
                    dve.tensor_tensor(a, a, b, ALU.add).then_inc(s_rope, 1)
                else:
                    dve.scalar_tensor_tensor(out=a, in0=a, scalar=rel_k0[:, 0:1], in1=b,
                                             op0=ALU.add, op1=ALU.add).then_inc(s_rope, 1)

            whole_program(dve, chunk, flush, run, prologue, split_expert)

        @block.gpsimd
        def _(pool):
            def lo(n_pass, k):
                n = CH * n_pass + k
                pool.wait_ge(s_hhi, n + 1)
                pool.tensor_tensor(hid_lo[:, k % 2, :], hid[:, k % 2, :], hid_hi[:, k % 2, :].bitcast(F32),
                                   ALU.subtract).then_inc(s_hlo, 1)

            def chunk(part, n_pass, k, second, ln, led):
                if part == 1 and led >= 1:
                    lo(*before(n_pass, k, 1))

            def flush(n_pass):
                lo(n_pass, CH - 1)

            def split_expert(e):
                pool.wait_ge(s_wsplit_hi, e + 1)
                pool.tensor_tensor(wg[:, LO, e, :], stage[e % 2][:, 0:F], wg[:, HI, e, :].bitcast(F32), ALU.subtract)
                pool.tensor_tensor(wu[:, LO, e, :], stage[e % 2][:, F:2 * F], wu[:, HI, e, :].bitcast(F32),
                                   ALU.subtract).then_inc(s_wsplit_lo, 1)

            def prologue():
                pool.wait_ge(s_half, 1)
                norm(0)

            def norm(m):
                pool.wait_ge(s_mom, m + 1)
                pool.tensor_tensor(var_eps[:, :], moments[:, :, 1], eps[:, :], ALU.add).then_inc(s_ve, 1)
                pool.wait_ge(s_ve, m + 1)
                pool.tensor_tensor(rstd[:, :], var_eps[:, :], minus_half[:, :], ALU.pow).then_inc(s_rstd, 1)

            def run(name, arg, t):
                if name in ("ln1a", "ln2a", "ln3a"):
                    norm(ln_index(name, t))
                if name in ("qhi", "khi"):
                    i = int(name == "khi")
                    pool.wait_ge(s_qkhi, 2 * t + i + 1)
                    pool.tensor_tensor(qk_r[:, 2 * i + 1, :], (Q1, K1)[i], qk[:, 2 * i, :],
                                       ALU.subtract).then_inc(s_qklo, 1)

                if name in ("vsplit1", "vsplit2"):
                    n = int(name[6]) - 1
                    pool.wait_ge(s_vhi, 2 * t + n + 1)
                    out = v_rows if n == 0 else v_b[:, 2, :, :]
                    pool.tensor_tensor(out, v_rows, v_b[:, n, :, :], ALU.subtract).then_inc(s_v, 1)
                if name == "turn" and 1 <= arg <= NU:
                    u = arg - 1
                    h, i = u // NT, u % NT
                    cols = (i + 1) * P
                    pool.wait_ge(s_phi, NU * t + u + 1)
                    pool.tensor_tensor(probs_16[:, u % PROBS_16, LO, 0:cols],
                                       probs[:, h % 2, R + i * L:R + i * L + cols],
                                       probs_16[:, u % PROBS_16, HI, 0:cols], ALU.subtract).then_inc(s_plo, 1)

            whole_program(pool, chunk, flush, run, prologue, split_expert)


_OUT = ((8, 512, 128), "float32")


def kernel(**inputs):
    import numpy as np
    import concourse.bacc as bacc
    from concourse import mybir
    from concourse.bass_utils import run_bass_kernel_spmd

    x = np.ascontiguousarray(inputs["L0_attn_x"])
    rel = np.asarray(inputs["L0_attn_rel_emb"])
    P, L, H, DH, R, HQ = 128, x.shape[1], 16, 8, 32, 4
    f32 = np.float32

    def dh_major(w):
        return np.asarray(w).reshape(H, DH, P).transpose(1, 0, 2)

    def swapped(w):
        return dh_major(w).reshape(DH // 2, 2, H, P)[:, ::-1].reshape(DH, H, P)

    order = np.array([HQ * (n % HQ) + n // HQ for n in range(H)])
    heads = np.asarray(inputs["L0_attn_w_v"]).reshape(H, DH, P)[order]
    w_o = np.asarray(inputs["L0_attn_w_o"]).reshape(P, H, DH)[:, order].reshape(P, P)
    watt = np.stack([m.reshape(P, P).T for m in (
        dh_major(inputs["L0_attn_w_q"]), swapped(inputs["L0_attn_w_q"]),
        dh_major(inputs["L0_attn_w_k"]), swapped(inputs["L0_attn_w_k"]), heads, w_o)], axis=1)

    rel_g, rel_g0 = np.zeros((HQ, 4, DH, HQ, R), rel.dtype), np.zeros((HQ, 4, DH, HQ, R), rel.dtype)
    rel_c, rel_c0 = np.zeros((HQ, R, HQ, DH), rel.dtype), np.zeros((HQ, R, HQ, DH), rel.dtype)
    for a in range(HQ):
        rel_g[a, :, :, a, :] = rel[1:R + 1].T
        rel_g0[a, :, :, a, :] = rel[0][:, None]
        rel_c[a, :, a, :] = rel[1:R + 1]
        rel_c0[a, :, a, :] = rel[0]

    inv_freq = 1.0 / 10000.0 ** (np.arange(0, DH, 2, dtype=f32) / DH)
    angle = np.outer(inv_freq.astype(f32), np.arange(L, dtype=f32)).astype(f32)
    cos = np.repeat(np.cos(angle.astype(np.float64)), 2, axis=0)
    sin = np.repeat(np.sin(angle.astype(np.float64)), 2, axis=0) * np.tile([-1.0, 1.0], DH // 2)[:, None]
    i, w = np.arange(P)[:, None], np.arange(P + R)[None, :]
    window = np.where(w > i + R, -1e30, 0.0)
    lanes = np.tile(np.repeat([[0.0, 1.0], [1.0, -1.0], [0.0, 1.0], [1.0, -1.0]], DH, axis=0), (HQ, 1))

    arrays = {
        "x": x, "wg": inputs["L0_ffn_Wg"], "wu": inputs["L0_ffn_Wu"], "wd": inputs["L0_ffn_Wd"],
        "watt": watt.reshape(P, -1), "rel_g": rel_g.reshape(P, P), "rel_g0": rel_g0.reshape(P, P),
        "rel_c": rel_c.reshape(P, R), "rel_c0": rel_c0.reshape(P, R),
        "rel_k0": np.repeat(rel[0], H)[:, None], "rel_v0": np.tile(rel[0], (P, H)),
        "cos": np.repeat(cos, H, axis=0).astype(f32), "sin": np.repeat(sin, H, axis=0).astype(f32),
        "window": window.astype(f32), "ident": np.eye(P, dtype=f32), "lanes": lanes.astype(f32),
    }
    nc = bacc.Bacc("TRN2", target_bir_lowering=False, num_devices=1)
    given, args = {}, []
    for name, a in arrays.items():
        a = np.ascontiguousarray(a)
        given[f"in_{name}"] = a
        args.append(nc.dram_tensor(f"in_{name}", a.shape, mybir.dt.from_np(a.dtype), kind="ExternalInput").ap())
    args.append(nc.dram_tensor("out", _OUT[0], mybir.dt.float32, kind="ExternalOutput").ap())
    macaron_kernel(nc, *args)
    return run_bass_kernel_spmd(nc, [given], core_ids=[0]).results[0]["out"]
```

```python
import concourse.bass as bass
from concourse import mybir
from contextlib import ExitStack


def macaron_kernel(nc, x_d, wg_d, wu_d, wd_d, watt_d, rel_g_d, rel_g0_d, rel_c_d, rel_c0_d,
                   rel_k0_d, rel_v0_d, cos_d, sin_d, window_d, ident_d, lanes_d, out_d):
    F32 = mybir.dt.float32
    F32R = mybir.dt.float32r
    F16 = mybir.dt.float16
    BF16 = mybir.dt.bfloat16
    ALU = mybir.AluOpType
    ACT = mybir.ActivationFunctionType
    AX = mybir.AxisListType

    P = 128
    B, L, D = x_d.shape
    E, _, F = wg_d.shape
    FC = F // P
    CH = E * FC
    NT = L // P
    H = 16
    DH = D // H
    R = 32
    HQ = 4
    HG = H // HQ
    W = P + R
    NU = H * NT
    QSCALE = -float(DH) ** -0.5
    EPS = 1e-5
    UP = 1
    TANH = 0
    GATED = 1
    PRODUCT = 2
    HID_HI = 4
    HID_LO = 4
    DOWN = 8
    REST_MAX = (0, 0)
    WINDOW = (0, 0)
    EXP = (2, 4)
    PROBS_HI = (4, 4)
    PROBS_LO = (4, 4)
    STORE = (8, 8)
    TURN = (12, 13)
    TURNED = (12, 13)
    VALUES = (16, 21)
    GROUP_SUM = (17, 16)
    BAND_TURN = (29, 28)
    BAND_TURNED = (29, 28)
    LAST_REL = (35, 32)
    LAST_REL_SUM = (30, 33)
    NORM2_AFTER = ((0, 1, 2, 2, 5, 7, 7, 8), (0, 1, 2, 2, 4, 6, 6, 6))
    PROJECT_AT = (11, 9)
    PROJECT_AFTER = ((0, 0, 2, 3, 3, 4, 6, 8, 10, 12),
                     (0, 0, 2, 3, 3, 4, 6, 6, 8, 10))
    NORM1_AT = 24
    NORM1_AFTER = (0, 4, 5, 6, 6)
    QREL_AT = 39
    QREL_AT_FIRST, QREL_AT_LAST = 28, 29
    QREL_AFTER = ((0, 0, 0, 0), (0, 0, 0, 0))
    UNITS_AT = 52
    UNITS_AT_FIRST, UNITS_AT_LAST = 36, 37
    OUTPUT_AT = 0
    CONTEXT_LEAD = 16
    CONTEXT_LEAD_FIRST, CONTEXT_LEAD_LAST = 0, 0
    CONTEXT_AFTER = ((0, 3, 3, 4, 6, 7, 7, 10, 12, 12, 13),
                     (0, 3, 3, 4, 6, 7, 7, 10, 12, 12, 13))
    NORM1_AFTER_FIRST = (0, 2, 6, 6, 6)
    PREPARE_AT, SECOND_NORM_AT, SPLIT_PART, LAST_OUTPUT_AT = 42, 51, 1, 4
    TILE = P * W
    HI, LO = 0, 1
    VP = 3
    PSCALE = 2.0 ** 15
    GU = HQ * NT
    HB = 4
    PROBS_16 = 3

    zwin_h = nc.dram_tensor("rel_window_scratch", [H * NT * TILE], F32, kind="Internal")
    pwin_h = nc.dram_tensor("prob_window_scratch", [H * NT * TILE], F32, kind="Internal")
    q_h = nc.dram_tensor("q_scratch", [4 * P * L], F32, kind="Internal")
    k_h = nc.dram_tensor("k_scratch", [4 * P * L], F32, kind="Internal")
    zwin_t, pwin_t, q_t, k_t = (h.ap().tensor for h in (zwin_h, pwin_h, q_h, k_h))

    ctx = ExitStack()
    with ctx:
        def sb(name, shape, dt=F32):
            return ctx.enter_context(nc.sbuf_tensor(name, shape, dt))

        def pb(name, shape):
            return ctx.enter_context(nc.psum_tensor(name, shape, F32))

        def sem(name):
            return ctx.enter_context(nc.semaphore(name))

        wg = sb("wg", [P, 2, E, F], F32R)
        wu = sb("wu", [P, 2, E, F], F32R)
        wd = sb("wd", [P, 2, E, F], F32R)
        watt = sb("watt", [P, 2, 6, P], F32R)
        WQ, WQS, WK, WKS, WV, WO = range(6)
        x0 = sb("x0", [P, L])
        x1 = sb("x1", [P, L])
        x2 = sb("x2", [P, L])
        xn = sb("xn", [P, L])
        xt1 = sb("xt1", [P, 2, L], F32R)
        xt2 = sb("xt2", [P, 2, L], F32R)
        acc_t = sb("acc_t", [P, L])
        out_s = xn
        hid = sb("hid", [P, HB, L])
        hid_hi = sb("hid_hi", [P, 2, L], F32R)
        hid_lo = sb("hid_lo", [P, 2, L], F32R)
        cos_s = sb("cos_s", [P, L])
        sin_s = sb("sin_s", [P, L])
        qq = sb("qq", [P, HG, L], F32R)
        kk = sb("kk", [P, HG, L], F32R)
        v_s = acc_t
        v_b = sb("v_b", [P, VP, NT, P], BF16)
        rel_win = sb("rel_win", [P, 3, NT, W])
        g_a = sb("g_a", [P, NT, H, R])
        probs = sb("probs", [P, 2, R + NT * L])
        probs_16 = sb("probs_16", [P, PROBS_16, 2, L], F16)
        probs_t = sb("probs_t", [P, 2, 2, L], F16)
        band_t = sb("band_t", [P, L])
        ctx_s = sb("ctx_s", [P, L])
        negmax = sb("negmax", [P, NU])
        denom = sb("denom", [P, NU])
        rdenom = sb("rdenom", [P, NU])
        rel_g = sb("rel_g", [P, P], F32R)
        rel_c = sb("rel_c", [P, R])
        rel_k0 = sb("rel_k0", [P, 1])
        rel_v0 = sb("rel_v0", [P, P])
        ident = sb("ident", [P, P])
        ident_16 = sb("ident_16", [P, P], F16)
        lanes = sb("lanes", [P, 2])
        stats = sb("stats", [P, NT, 6])
        moments = sb("moments", [P, NT, 2])
        var_eps = sb("var_eps", [P, NT])
        rstd = sb("rstd", [P, NT])
        minus_half = sb("minus_half", [P, NT])
        eps = sb("eps", [P, NT])
        settled = sb("settled", [P, 1])

        rope = [probs[:, 0, R + i * L:R + (i + 1) * L] for i in range(4)]
        Q1, Q2, K1, K2 = rope
        qk = probs[:, 1, R:].rearrange("p (c l) -> p c l", c=4)
        qk_r = qk.bitcast(F32R)
        stage = [probs[:, i, R:R + 3 * F] for i in range(2)]
        raw_att = g_a[:, :, :, :].rearrange("p a b c -> p (a b c)")[:, 0:6 * P]
        raw_rel = g_a[:, :, :, :].rearrange("p a b c -> p (a b c)")[:, 6 * P:6 * P + 2 * P + 2 * R]
        window = rel_win[:, 0, 0, :]
        v_rows = v_s[:, :].rearrange("p (a b) -> p a b", a=NT)

        hidden = [pb(f"hidden{i}", [P, L]) for i in range(3)]
        acc = pb("acc", [P, L])
        work = [pb(f"work{i}", [P, L]) for i in range(3)]
        ctx_p = pb("ctx_p", [P, L])
        turned = work[2][:, :].bitcast(F16).rearrange("p (a b) -> p a b", a=2)
        summed = ctx_p[:, 0:GU * VP * DH]
        rel_sum = ctx_p[:, GU * VP * DH:GU * (VP + 1) * DH]

        s_wgate = [sem(f"expert_gate_loaded{i}") for i in range(2)]
        s_wup = [sem(f"expert_up_loaded{i}") for i in range(2)]
        s_wdown = [sem(f"expert_down_loaded{i}") for i in range(2)]
        s_ident = sem("ident_loaded")
        s_wsplit_hi = sem("expert_hi")
        s_wsplit_lo = sem("expert_up_lo")
        s_wsplit_dlo = sem("expert_down_lo")
        s_const = sem("constants_loaded")
        s_win = sem("window_loaded")
        s_half = sem("exponent_set")
        s_att_hi = sem("att_weights_hi")
        s_att_lo = sem("att_weights_lo")
        s_rel = sem("rel_prepared")
        s_gate = sem("gate_ready")
        s_up = sem("up_ready")
        s_tanh = sem("tanh_ready")
        s_act = sem("gated_ready")
        s_hid = sem("hid_ready")
        s_hhi = sem("hid_hi_ready")
        s_hlo = sem("hid_lo_ready")
        s_down = sem("down_done")
        s_acc = sem("acc_copied")
        s_ftok = sem("ffn_tokens")
        s_sum = sem("residual_summed")
        s_st = sem("stats_done")
        s_mom = sem("moments_ready")
        s_ve = sem("var_eps_ready")
        s_rstd = sem("rstd_ready")
        s_xn = sem("xn_ready")
        s_xnt = sem("xn_transposed")
        s_xhi = sem("xt_hi_ready")
        s_xlo = sem("xt_lo_ready")
        s_vhi = sem("v_part_ready")
        s_id16 = sem("ident_16_ready")
        s_proj = sem("projected")
        s_rope = sem("rope_step")
        s_qkhi = sem("qk_hi_ready")
        s_qklo = sem("qk_lo_ready")
        s_v = sem("v_step")
        s_qkst = [sem(f"{x}_stored") for x in "qk"]
        s_qkld = sem("qk_loaded")
        s_g = sem("qrel_done")
        s_gev = sem("qrel_copied")
        s_gst = sem("qrel_stored")
        s_z = [sem(f"window_of_head_loaded{i}") for i in range(3)]
        s_sc = sem("scores_ready")
        s_rest = sem("max_of_rest_ready")
        s_max = sem("max_ready")
        s_exp = sem("probs_ready")
        s_phi = sem("probs_hi_ready")
        s_plo = sem("probs_lo_ready")
        s_pt = sem("probs_transposed")
        s_ptc = sem("probs_t_copied")
        s_pv = sem("pv_done")
        s_pst = [sem(f"prob_window_stored{i}") for i in range(2)]
        s_band = [sem(f"bands_of_group_loaded{i}") for i in range(HG)]
        s_bt = sem("band_transposed")
        s_btc = sem("band_t_copied")
        s_crel = sem("ctx_rel_ready")
        s_rc = sem("ctx_rel_added")
        s_cc = sem("ctx_of_group_summed")
        s_cn = sem("ctx_step")
        s_ct = sem("ctx_transposed")
        s_chi = sem("ctx_t_hi")
        s_clo = sem("ctx_t_lo")
        s_o = sem("attention_out")
        s_x2 = sem("attention_summed")
        s_x = sem("x_loaded")
        s_xb = sem("second_batch_loaded")
        s_out = sem("dram_filled_then_outputs_stored")

        x_v = x_d.rearrange("b (t p) d -> b p t d", p=P)
        out_v = out_d.rearrange("b (t p) d -> b p t d", p=P)

        def ctx_t(t):
            return xt1 if isinstance(t, int) else xt2

        def x2_of(t):
            return x0 if isinstance(t, int) and t == B - 1 else x2

        def column(h, i):
            return i * H + h

        def wait(eng, semaphore, value):
            if not (isinstance(value, int) and value <= 0):
                eng.wait_ge(semaphore, value)

        NORM2 = ("acc1", "sum1", "add1", "ln2a", "ln2b", "ln2t", "ln2h", "ln2c")
        PROJECT = ("proj1", "rot1", "proj2", "qhi", "rot2", "proj3", "khi", "vadd", "vsplit1", "vsplit2")
        NORM1 = ("ln1a", "ln1b", "ln1t", "ln1h", "ln1c")
        QREL = ("qrel1", "qrelcopy1", "qrel2", "qrelcopy2")
        CONTEXT = ("scale", "ctxt", "ctxhi", "ctxlo", "outproj", "attsum", "ln3a", "ln3b", "ln3t", "ln3h", "ln3c")

        FULL = 2 * 3 * CH

        def plan(parts, lists, first, last, context_after, out_at):
            pieces = [[] for _ in range(parts + 1)]

            def put(names, at, afters):
                for name, after in zip(names, afters):
                    waits_for_end = parts < FULL and name in ("ln3t", "ln3h", "ln3c")
                    pieces[parts if waits_for_end else min(at + after, parts)].append((name, 0))

            for names, at, afters in lists:
                put(names, at, afters)
            quarters = 4 * NU + max(LAST_REL_SUM)
            for n in range(quarters):
                pieces[first + n * (last - first) // quarters].append(("quarter", n))
            put(CONTEXT, min(last + 1, parts), context_after)
            if out_at == parts:
                pieces[parts].insert(0, ("acc2", 0))
            elif out_at is not None:
                pieces[out_at].append(("acc2", 0))
                for slot in pieces[out_at + 2:]:
                    units = [i for i, (name, u) in enumerate(slot) if name == "quarter" and u % 8 == 0]
                    if units:
                        u = slot[units[0]][1]
                        slot[units[0]:units[0] + 1] = [("sum2", u), ("add2", 0), ("quarter_after_sum2", u)]
                        break
            return pieces

        START = DOWN - 3
        SINGLE = 3 * CH
        FULL_STEP = plan(FULL, [(NORM2, START, NORM2_AFTER[0]), (PROJECT, START + PROJECT_AT[0], PROJECT_AFTER[0]),
                                (NORM1, START + NORM1_AT, NORM1_AFTER), (QREL, START + QREL_AT, QREL_AFTER[0])],
                         START + UNITS_AT, FULL - CONTEXT_LEAD, CONTEXT_AFTER[0], FULL // 2 + START + OUTPUT_AT)
        FIRST_STEP = plan(SINGLE, [(NORM2, START, NORM2_AFTER[1]),
                                   (PROJECT, START + PROJECT_AT[1], PROJECT_AFTER[1]),
                                   (QREL, START + QREL_AT_FIRST, QREL_AFTER[1])],
                          START + UNITS_AT_FIRST, SINGLE - CONTEXT_LEAD_FIRST, CONTEXT_AFTER[1], None)
        LAST_STEP = plan(SINGLE, [(NORM2, START, NORM2_AFTER[1]),
                                  (PROJECT, START + PROJECT_AT[1], PROJECT_AFTER[1]),
                                  (QREL, START + QREL_AT_LAST, QREL_AFTER[1])],
                         START + UNITS_AT_LAST, SINGLE - CONTEXT_LEAD_LAST, CONTEXT_AFTER[1], SINGLE)
        FIRST_PASS = {PREPARE_AT: (("prepare", 0),)}
        for name, after in zip(NORM1, NORM1_AFTER_FIRST):
            at = SECOND_NORM_AT + after
            FIRST_PASS[at] = FIRST_PASS.get(at, ()) + ((name, 0),)
        LAST_PASS = {LAST_OUTPUT_AT: (("sum2", 4 * NU + 4),), LAST_OUTPUT_AT + 2: (("add2", 0),)}

        def ln_index(name, t):
            if isinstance(t, int) and t == 0:
                return {"ln1": 1, "ln2": 2, "ln3": 3}[name[:3]]
            after_ln2 = 1 if not isinstance(t, int) or t < B - 1 else 0
            return 3 * t + 1 + {"ln2": 0, "ln1": 1, "ln3": 1 + after_ln2}[name[:3]]

        def sum_index(name, t):
            first = 2 * t - 1 if not isinstance(t, int) or t > 0 else 0
            return {"1": first, "2": 2 * t, "t": 2 * B - 1}[name[-1]]

        def before(n_pass, k, j):
            return (n_pass, k - j) if k >= j else (n_pass - 1, CH + k - j)

        assert CH % 3 == 2

        def gate_bank(k):
            return hidden[2 * k % 3]

        def up_bank(k):
            return hidden[(2 * min(k, CH - 2) + 1) % 3]

        def behind(part, offset, k, led):
            j, rest = divmod(offset - part, 3)
            return j if rest == 0 and 0 <= j <= led and k - j < CH else None

        def due(n, offsets, t):
            u, rest = divmod(n - offsets[isinstance(t, int)], 4)
            return u if rest == 0 and 0 <= u < NU else None

        def group_due(n, offsets, t):
            u = due(n, offsets, t)
            return u // GU if u is not None and (u + 1) % GU == 0 else None

        def turned_by(n, t):
            return max(0, min(NU, (n - TURN[isinstance(t, int)]) // 4 + 1))

        def whole_program(eng, chunk, run, prologue, split_expert):
            def flush(n_pass, second):
                for k in range(CH, CH + DOWN // 3 + 1):
                    for part in range(3):
                        chunk(part, n_pass, k, second, 0, CH)

            def passes(t, order, pieces):
                for m, (n_pass, second, ln, led) in enumerate(order):
                    for k in range(CH):
                        for part in range(3):
                            chunk(part, n_pass, k, second, ln, min(led + k, CH))
                            for name, arg in pieces[3 * (CH * m + k) + part]:
                                run(name, arg, t)

            prologue()
            for piece in range(3):
                split_expert(0, piece)
            for k in range(CH):
                for part in range(3):
                    chunk(part, 0, k, False, 0, k)
                    for name, arg in FIRST_PASS.get(3 * k + part, ()):
                        run(name, arg, 0)
                    if part == SPLIT_PART and k % FC < 3 and k // FC + 1 < E:
                        split_expert(k // FC + 1, k % FC)
            pieces = FIRST_STEP
            passes(0, [(1, True, ln_index("ln1", 0), CH)], pieces)
            for name, arg in pieces[3 * CH]:
                run(name, arg, 0)
            with eng.Fori(1, B - 1) as t:
                pieces = FULL_STEP
                passes(t, [(2 * t, True, 3 * t, CH), (2 * t + 1, False, ln_index("ln1", t), CH)], pieces)
                for name, arg in pieces[2 * 3 * CH]:
                    run(name, arg, t)
            t = B - 1
            pieces = LAST_STEP
            passes(t, [(2 * t, True, 3 * t, CH)], pieces)
            flush(2 * t, True)
            for name, arg in pieces[3 * CH]:
                run(name, arg, t)
            for k in range(CH):
                for part in range(3):
                    chunk(part, 2 * B - 1, k, True, ln_index("ln3", t), k)
                    for name, arg in LAST_PASS.get(3 * k + part, ()):
                        run(name, arg, t)
            flush(2 * B - 1, True)
            for name in ("acclast", "sumlast", "addlast"):
                run(name, 0, B)

        block = ctx.enter_context(nc.Block())

        @block.sync
        def _(sp):
            def no_chunk(part, n_pass, k, second, ln, led):
                pass

            def no_split(e, piece):
                pass

            def prologue():
                sp.dma_start(x0[:, :].rearrange("p (t d) -> p t d", t=NT), x_v[0]).then_inc(s_x, 16)
                sp.dma_start(ident[:, :], ident_d).then_inc(s_ident, 16)
                for e in range(2):
                    load_expert(e)
                sp.dma_start(window, window_d).then_inc(s_win, 16)
                for dst, src in ((raw_att, watt_d), (cos_s[:, :], cos_d), (sin_s[:, :], sin_d),
                                 (rel_k0[:, :], rel_k0_d), (rel_v0[:, :], rel_v0_d), (lanes[:, :], lanes_d),
                                 (raw_rel[:, 0:P], rel_g_d), (raw_rel[:, P:2 * P], rel_g0_d),
                                 (raw_rel[:, 2 * P:2 * P + R], rel_c_d), (raw_rel[:, 2 * P + R:], rel_c0_d)):
                    sp.dma_start(dst, src).then_inc(s_const, 16)
                sp.dma_start(x2[:, :].rearrange("p (t d) -> p t d", t=NT), x_v[1]).then_inc(s_xb, 16)
                for e in range(2, E):
                    sp.wait_ge(s_wsplit_hi, 3 * (e - 1))
                    sp.wait_ge(s_wsplit_lo, 2 * (e - 1))
                    sp.wait_ge(s_wsplit_dlo, e - 1)
                    load_expert(e)
                sp.wait_ge(s_win, 16)
                sp.dma_start(bass.AP(zwin_t, 0, [[W, P], [TILE, H * NT], [1, W]]),
                             window[:, None, :].to_broadcast([P, H * NT, W])).then_inc(s_out, 16)
                sp.wait_ge(s_out, 16)

            def load_expert(e):
                dst = stage[e % 2]
                sp.dma_start(dst[:, 0:F], wg_d[e]).then_inc(s_wgate[e % 2], 16)
                sp.dma_start(dst[:, F:2 * F], wu_d[e]).then_inc(s_wup[e % 2], 16)
                sp.dma_start(dst[:, 2 * F:3 * F].rearrange("p (c d) -> p c d", c=FC),
                             wd_d[e].rearrange("(c p) d -> p c d", p=P)).then_inc(s_wdown[e % 2], 16)

            def load_window(h, t):
                if h >= 3:
                    sp.wait_ge(s_max, NU * t + NT * (h - 2))
                sp.dma_start(rel_win[:, h % 3, :, :],
                             bass.AP(zwin_t, h * NT * TILE, [[W, P], [TILE, NT], [1, W]])).then_inc(s_z[h % 3], 16)

            def run(name, arg, t):
                if name == "add1" and (not isinstance(t, int) or t < B - 1):
                    sp.wait_ge(s_sum, sum_index("sum1", t) + 1)
                    sp.dma_start(x0[:, :].rearrange("p (t d) -> p t d", t=NT),
                                 x_v[t + 1]).then_inc(s_x, 16)
                if name in ("qhi", "khi"):
                    k = int(name == "khi")
                    scratch, dst = ((q_t, qq), (k_t, kk))[k]
                    sp.wait_ge(s_qkhi, 2 * t + 1 + k)
                    sp.wait_ge(s_qklo, 2 * t + 1 + k)
                    for copy in range(2):
                        sp.dma_start(bass.AP(scratch, copy * (1 + k) * P * L, [[L, P], [(2 - k) * P * L, 2], [1, L]]),
                                     qk[:, 2 * k:2 * k + 2, :]).then_inc(s_qkst[k], 16)
                    sp.wait_ge(s_qkst[k], 32 * (t + 1))
                    sp.dma_start(dst[:, :, :].bitcast(F32).rearrange("p g l -> p (g l)"),
                                 bass.AP(scratch, 0, [[HG * L, HQ], [H * L, 4 * DH], [1, HG * L]])
                                 ).then_inc(s_qkld, 16)
                if name == "qrel2":
                    for i in range(NT):
                        sp.wait_ge(s_gev, NT * t + i + 1)
                        sp.dma_start(bass.AP(zwin_t, i * TILE + 1, [[W + 1, P], [NT * TILE, H], [1, R]]),
                                     g_a[:, i, :, :]).then_inc(s_gst, 16)
                    sp.wait_ge(s_gst, 16 * NT * (t + 1))
                    for h in range(2):
                        load_window(h, t)
                if name[:7] == "quarter" and arg % (4 * NT) == 0 and arg // (4 * NT) + 2 < H:
                    load_window(arg // (4 * NT) + 2, t)
                u = due(arg, STORE, t) if name[:7] == "quarter" else None
                if u is not None and u % NT == NT - 1:
                    h = u // NT
                    if h < H:
                        sp.wait_ge(s_exp, NU * t + NT * (h + 1))
                        sp.dma_start(bass.AP(pwin_t, h * NT * TILE, [[W, P], [TILE, NT], [1, W]]),
                                     bass.AP(probs[:, h % 2, :].tensor, probs[:, h % 2, :].offset,
                                             [list(probs[:, h % 2, :].ap[0]), [L + P, NT], [1, W]])
                                     ).then_inc(s_pst[h % 2], 16)
                        sp.wait_ge(s_pst[h % 2], 16 * (H // 2) * t + 16 * (h // 2 + 1))
                        sp.dma_start(g_a[:, :, h, :],
                                     bass.AP(pwin_t, h * NT * TILE + 1, [[W + 1, P], [TILE, NT], [1, R]])
                                     ).then_inc(s_band[h // HQ], 16)
                if name == "add2":
                    sp.wait_ge(s_sum, sum_index("sum2", t) + 1)
                    sp.dma_start(out_v[t - 1], out_s[:, :].rearrange("p (t d) -> p t d", t=NT)).then_inc(s_out, 16)
                if name == "addlast":
                    sp.wait_ge(s_sum, 2 * B)
                    sp.dma_start(out_v[B - 1], out_s[:, :].rearrange("p (t d) -> p t d", t=NT)).then_inc(s_out, 16)
                    sp.wait_ge(s_out, 16 * (B + 1))

            whole_program(sp, no_chunk, run, prologue, no_split)

        @block.tensor
        def _(pe):
            def three(out, w_hi, w_lo, m_hi, m_lo, start=True, stop=True):
                pe.matmul(out, w_hi, m_hi, start=start, stop=False)
                pe.matmul(out, w_hi, m_lo, start=False, stop=False)
                return pe.matmul(out, w_lo, m_hi, start=False, stop=stop)

            def transposes(dst, src, n=NT):
                for i in range(n):
                    last = pe.transpose(dst[:, i * P:(i + 1) * P], src[:, i * P:(i + 1) * P], ident[:, :])
                return last

            def down(n_pass, k):
                n = CH * n_pass + k
                e, c = k // FC, k % FC
                if isinstance(n_pass, int) and n_pass == 0 and c == 0:
                    pe.wait_ge(s_wsplit_hi, 3 * e + 3)
                    pe.wait_ge(s_wsplit_dlo, e + 1)
                pe.wait_ge(s_hhi, n + 1)
                pe.wait_ge(s_hlo, n + 1)
                if k == 0:
                    wait(pe, s_acc, n_pass)
                three(acc[:, :], wd[:, HI, e, c * P:(c + 1) * P], wd[:, LO, e, c * P:(c + 1) * P],
                      hid_hi[:, k % 2, :], hid_lo[:, k % 2, :],
                      start=(k == 0), stop=(k == CH - 1)).then_inc(s_down, 1)

            def up_projection(n_pass, k, second):
                n = CH * n_pass + k
                e, c = k // FC, k % FC
                xt = xt2 if second else xt1
                if isinstance(n_pass, int) and n_pass == 0 and c == 0:
                    pe.wait_ge(s_wsplit_hi, 3 * e + 2)
                    pe.wait_ge(s_wsplit_lo, 2 * e + 2)
                if k in (0, CH - 1):
                    wait(pe, s_hid, n)
                else:
                    wait(pe, s_act, n)
                three(up_bank(k)[:, :], wu[:, HI, e, c * P:(c + 1) * P], wu[:, LO, e, c * P:(c + 1) * P],
                      xt[:, HI, :], xt[:, LO, :]).then_inc(s_up, 1)

            def gate_projection(n_pass, k, second, ln):
                n = CH * n_pass + k
                e, c = k // FC, k % FC
                xt = xt2 if second else xt1
                if isinstance(n_pass, int) and n_pass == 0 and c == 0:
                    pe.wait_ge(s_wsplit_hi, 3 * e + 1)
                    pe.wait_ge(s_wsplit_lo, 2 * e + 1)
                if k == 0:
                    pe.wait_ge(s_xhi, ln + 1)
                    pe.wait_ge(s_xlo, ln + 1)
                wait(pe, s_hid, n - 1)
                three(gate_bank(k)[:, :], wg[:, HI, e, c * P:(c + 1) * P], wg[:, LO, e, c * P:(c + 1) * P],
                      xt[:, HI, :], xt[:, LO, :]).then_inc(s_gate, 1)

            def chunk(part, n_pass, k, second, ln, led):
                if part == 0 and k < CH:
                    gate_projection(n_pass, k, second, ln)
                if part == UP and k < CH:
                    up_projection(n_pass, k, second)
                j = behind(part, DOWN, k, led)
                if j is not None:
                    down(*before(n_pass, k, j))

            def prologue():
                pe.wait_ge(s_ident, 16)
                pe.wait_ge(s_xn, 1)
                transposes(work[1], xn).then_inc(s_xnt, 1)

            def no_split(e, piece):
                pass

            def run(name, arg, t):
                if name[:3] == "sum":
                    j = 2 * B - 1 if name == "sumlast" else sum_index(name, t)
                    pe.wait_ge(s_acc, j + 1)
                    if name == "sum2":
                        pe.wait_ge(s_exp, NU * t + arg // 4 - 1)
                    transposes(work[0], acc_t).then_inc(s_ftok, 1)
                if name in ("ln1t", "ln2t", "ln3t"):
                    pe.wait_ge(s_xn, ln_index(name, t) + 1)
                    transposes(work[1], xn).then_inc(s_xnt, 1)
                if name == "proj1":
                    if isinstance(t, int) and t == 0:
                        pe.wait_ge(s_id16, 1)
                        pe.wait_ge(s_att_hi, 1)
                        pe.wait_ge(s_att_lo, 1)
                    pe.wait_ge(s_xhi, ln_index("ln2", t) + 1)
                    pe.wait_ge(s_xlo, ln_index("ln2", t) + 1)
                    for w, bank in ((WQ, work[0]), (WQS, ctx_p)):
                        three(bank[:, :], watt[:, HI, w, :], watt[:, LO, w, :],
                              xt1[:, HI, :], xt1[:, LO, :]).then_inc(s_proj, 1)
                if name == "proj2":
                    three(work[1][:, :], watt[:, HI, WK, :], watt[:, LO, WK, :],
                          xt1[:, HI, :], xt1[:, LO, :]).then_inc(s_proj, 1)
                    three(work[2][:, :], watt[:, HI, WKS, :], watt[:, LO, WKS, :],
                          xt1[:, HI, :], xt1[:, LO, :]).then_inc(s_proj, 1)
                if name == "proj3":
                    pe.wait_ge(s_rope, 6 * t + 2)
                    for i in range(NT):
                        cols = slice(i * P, (i + 1) * P)
                        last = three(ctx_p[:, cols], xt1[:, HI, cols], xt1[:, LO, cols],
                                     watt[:, HI, WV, :], watt[:, LO, WV, :])
                    last.then_inc(s_proj, 1)
                if name == "qrel1":
                    pe.wait_ge(s_qkld, 32 * (t + 1))
                    pe.wait_ge(s_rope, 6 * t + 5)
                    if isinstance(t, int) and t == 0:
                        pe.wait_ge(s_rel, 3)
                    pe.wait_ge(s_v, VP * t + 1)
                if name in ("qrel1", "qrel2"):
                    for i in range(2):
                        bank = (work[0], ctx_p)[i]
                        tile = i + 2 * (name == "qrel2")
                        if name == "qrel2":
                            pe.wait_ge(s_gev, NT * t + i + 1)
                        for g in range(HG):
                            last = pe.matmul(bank[:, g * P:(g + 1) * P], qq[:, g, tile * P:(tile + 1) * P],
                                             rel_g[:, :], start=True, stop=True)
                        last.then_inc(s_g, 1)
                if name == "quarter_after_sum2":
                    pe.wait_ge(s_sum, sum_index("sum2", t) + 1)
                if name[:7] == "quarter":
                    for offset, stage_of in (((0, 0), scores), (VALUES, context_of), (TURN, turn)):
                        u = due(arg, offset, t)
                        if u is not None:
                            stage_of(u, t)
                    g = group_due(arg, BAND_TURN, t)
                    if g is not None:
                        turn_bands(g, arg, t)
                    if group_due(arg, LAST_REL, t) == HG - 1:
                        pe.wait_ge(s_cc, HG * (t + 1))
                        context_rel(HG - 1, t)
                if name == "ctxt":
                    pe.wait_ge(s_cn, 2 * t + 2)
                    transposes(work[0], ctx_s).then_inc(s_ct, 1)
                if name == "outproj":
                    pe.wait_ge(s_chi, t + 1)
                    pe.wait_ge(s_clo, t + 1)
                    for i in range(NT):
                        cols = slice(i * P, (i + 1) * P)
                        last = three(work[1][:, cols], ctx_t(t)[:, HI, cols], ctx_t(t)[:, LO, cols],
                                     watt[:, HI, WO, :], watt[:, LO, WO, :])
                    last.then_inc(s_o, 1)

            def scores(u, t):
                h, i = u // NT, u % NT
                a, g = h % HQ, h // HQ
                rows = slice(32 * a, 32 * a + 32)
                if u == 0:
                    pe.wait_ge(s_gev, NT * t + NT)
                if u == 1:
                    last_ln = "ln2" if isinstance(t, int) else "ln1"
                    pe.wait_ge(s_xlo, ln_index(last_ln, t) + 1)
                if u >= 2:
                    pe.wait_ge(s_exp, NU * t + u - 1)
                cols = (i + 1) * P
                pe.matmul(work[u % 2][:, 0:cols], qq[rows, g, i * P:(i + 1) * P], kk[rows, g, 0:cols],
                          start=True, stop=True).then_inc(s_sc, 1)

            def context_of(u, t):
                h, i = u // NT, u % NT
                pe.wait_ge(s_ptc, NU * t + u + 1)
                if u == 0:
                    pe.wait_ge(s_v, VP * t + VP)
                    pe.wait_ge(s_vhi, 2 * t + 2)
                elif u % GU == 0:
                    pe.wait_ge(s_cc, HG * t + u // GU)
                o = (i * HQ + h % HQ) * VP * DH
                for j in range(i + 1):
                    for part in (HI, LO):
                        last = pe.matmul(ctx_p[:, o:o + VP * DH], probs_t[:, u % 2, part, j * P:(j + 1) * P],
                                         v_b[:, :, j, h * DH:(h + 1) * DH],
                                         start=(j == 0 and part == HI), stop=(j == i and part == LO))
                last.then_inc(s_pv, 1)
                if (u + 1) % GU == 0 and u >= GU:
                    context_rel(u // GU - 1, t)

            def turn(u, t):
                pe.wait_ge(s_plo, NU * t + u + 1)
                if u >= 1:
                    pe.wait_ge(s_ptc, NU * t + u)
                for g in range(HG):
                    if turned_by(4 * (GU * (g + 1) - 1) + BAND_TURN[isinstance(t, int)], t) == u:
                        pe.wait_ge(s_btc, HG * t + g + 1)
                for part in (HI, LO):
                    for j in range(u % NT + 1):
                        last = pe.transpose(turned[:, part, j * P:(j + 1) * P],
                                            probs_16[:, u % PROBS_16, part, j * P:(j + 1) * P], ident_16[:, :])
                last.then_inc(s_pt, 1)

            def turn_bands(g, n, t):
                pe.wait_ge(s_band[g], 16 * HQ * (t + 1))
                pe.wait_ge(s_ptc, NU * t + turned_by(n, t))
                for i in range(NT):
                    last = pe.transpose(work[2][:, i * P:(i + 1) * P],
                                        g_a[:, i, g * HQ:(g + 1) * HQ, :].rearrange("p h r -> p (h r)"),
                                        ident[:, :])
                last.then_inc(s_bt, 1)

            def context_rel(g, t):
                pe.wait_ge(s_btc, HG * t + g + 1)
                for i in range(NT):
                    last = pe.matmul(rel_sum[:, i * HQ * DH:(i + 1) * HQ * DH], band_t[:, i * P:(i + 1) * P],
                                     rel_c[:, :], start=True, stop=True)
                last.then_inc(s_crel, 1)

            whole_program(pe, chunk, run, prologue, no_split)

        @block.scalar
        def _(act):
            def hi(n_pass, k):
                n = CH * n_pass + k
                act.wait_ge(s_hid, n + 1)
                wait(act, s_down, n - 1)
                act.copy(hid_hi[:, k % 2, :], hid[:, k % HB, :]).then_inc(s_hhi, 1)

            def tanh(n_pass, k):
                n = CH * n_pass + k
                act.wait_ge(s_gate, n + 1)
                wait(act, s_hlo, n + 1 - HB)
                act.activation(hid[:, k % HB, :], gate_bank(k)[:, :], ACT.Tanh, scale=0.5).then_inc(s_tanh, 1)

            def chunk(part, n_pass, k, second, ln, led):
                for offset, stage_of in ((TANH, tanh), (HID_HI, hi)):
                    j = behind(part, offset, k, led)
                    if j is not None:
                        stage_of(*before(n_pass, k, j))

            def split_expert(e, piece):
                loaded = (s_wgate, s_wup, s_wdown)[piece][e % 2]
                act.wait_ge(loaded, 16 * (e // 2 + 1))
                act.copy((wg, wu, wd)[piece][:, HI, e, :],
                         stage[e % 2][:, piece * F:(piece + 1) * F]).then_inc(s_wsplit_hi, 1)

            def prologue():
                act.wait_ge(s_xnt, 1)
                act.copy(xt1[:, HI, :], work[1][:, :]).then_inc(s_xhi, 1)

            def prepare():
                act.wait_ge(s_const, 16 * 10)
                act.wait_ge(s_ident, 16)
                act.copy(ident_16[:, :], ident[:, :]).then_inc(s_id16, 1)
                act.copy(watt[:, HI, :, :].rearrange("p a b -> p (a b)"), raw_att).then_inc(s_att_hi, 1)

            def run(name, arg, t):
                if name == "prepare":
                    prepare()
                if name[:3] == "acc":
                    j = 2 * B - 1 if name == "acclast" else sum_index(name, t)
                    act.wait_ge(s_down, CH * (j + 1))
                    wait(act, s_ftok, j)
                    act.mul(acc_t[:, :], acc[:, :], 0.25).then_inc(s_acc, 1)
                if name in ("ln1h", "ln2h", "ln3h"):
                    second_batch = isinstance(t, int) and t == 0 and name == "ln1h"
                    xt = xt2 if name == "ln3h" or second_batch else xt1
                    act.wait_ge(s_xnt, ln_index(name, t) + 1)
                    act.copy(xt[:, HI, :], work[1][:, :]).then_inc(s_xhi, 1)
                if name in ("qhi", "khi"):
                    i = int(name == "khi")
                    act.wait_ge(s_rope, 6 * t + 3 * (i + 1))
                    act.copy(qk_r[:, 2 * i, :], (Q1, K1)[i]).then_inc(s_qkhi, 1)
                if name in ("qrelcopy1", "qrelcopy2"):
                    for i in range(2):
                        tile = i + 2 * (name == "qrelcopy2")
                        act.wait_ge(s_g, NT * t + tile + 1)
                        act.copy(g_a[:, tile, :, :].rearrange("p h r -> p (h r)"),
                                 (work[0], ctx_p)[i][:, :]).then_inc(s_gev, 1)
                if name[:7] == "quarter":
                    for offset, stage_of in ((EXP, exponentials), (TURNED, copy_turned)):
                        u = due(arg, offset, t)
                        if u is not None:
                            stage_of(u, t)
                    g = group_due(arg, BAND_TURNED, t)
                    if g is not None:
                        act.wait_ge(s_bt, HG * t + g + 1)
                        if g > 0:
                            act.wait_ge(s_crel, HG * t + g)
                        act.copy(band_t[:, :], work[2][:, :]).then_inc(s_btc, 1)
                if name in ("vsplit1", "vsplit2"):
                    n = int(name[6]) - 1
                    act.wait_ge(s_v, VP * t + n + 1)
                    act.copy(v_b[:, n, :, :], v_rows).then_inc(s_vhi, 1)
                if name == "ctxhi":
                    act.wait_ge(s_ct, t + 1)
                    act.copy(ctx_t(t)[:, HI, :], work[0][:, :]).then_inc(s_chi, 1)

            def copy_turned(u, t):
                cols = (u % NT + 1) * P
                act.wait_ge(s_pt, NU * t + u + 1)
                if u >= 2:
                    act.wait_ge(s_pv, NU * t + u - 1)
                act.mul(probs_t[:, u % 2, :, 0:cols], turned[:, :, 0:cols], PSCALE).then_inc(s_ptc, 1)

            def exponentials(u, t):
                h, i = u // NT, u % NT
                act.wait_ge(s_max, NU * t + u + 1)
                if i == 0 and h >= 2:
                    act.wait_ge(s_pst[h % 2], 16 * (H // 2) * t + 16 * (h // 2))
                if u == 0:
                    act.wait_ge(s_qkst[0], 32 * (t + 1))
                    act.wait_ge(s_qkst[1], 32 * (t + 1))
                c = column(h, i)
                act.activation(probs[:, h % 2, R + i * L:R + i * L + (i + 1) * P],
                               work[u % 2][:, 0:(i + 1) * P], ACT.Exp,
                               scale=-1.0, bias=negmax[:, c:c + 1], accum_out=denom[:, c:c + 1]).then_inc(s_exp, 1)

            whole_program(act, chunk, run, prologue, split_expert)

        @block.vector
        def _(dve):
            def product(n_pass, k):
                n = CH * n_pass + k
                dve.wait_ge(s_act, n + 1)
                dve.wait_ge(s_up, n + 1)
                dve.tensor_tensor(hid[:, k % HB, :], hid[:, k % HB, :], up_bank(k)[:, :], ALU.mult).then_inc(s_hid, 1)

            def gated(n_pass, k):
                n = CH * n_pass + k
                dve.wait_ge(s_tanh, n + 1)
                dve.scalar_tensor_tensor(out=hid[:, k % HB, :], in0=hid[:, k % HB, :], scalar=1.0,
                                         in1=gate_bank(k)[:, :], op0=ALU.add, op1=ALU.mult).then_inc(s_act, 1)

            def chunk(part, n_pass, k, second, ln, led):
                for offset, stage_of in ((GATED, gated), (PRODUCT, product)):
                    j = behind(part, offset, k, led)
                    if j is not None:
                        stage_of(*before(n_pass, k, j))

            def split_expert(e, piece):
                if piece < 2:
                    return
                dve.wait_ge(s_wsplit_hi, 3 * e + 3)
                dve.tensor_tensor(wd[:, LO, e, :], stage[e % 2][:, 2 * F:3 * F],
                                  wd[:, HI, e, :].bitcast(F32), ALU.subtract).then_inc(s_wsplit_dlo, 1)

            def prologue():
                dve.memset(minus_half[:, :], -0.5)
                dve.memset(eps[:, :], EPS).then_inc(s_half, 1)
                dve.memset(probs[:, :, 0:R], 0.0)
                dve.wait_ge(s_x, 16)
                norm_a(0, x0)
                norm_b(0, x0)
                norm_c(0, xt1)

            def prepare():
                dve.wait_ge(s_const, 16 * 10)
                dve.wait_ge(s_att_hi, 1)
                dve.tensor_tensor(watt[:, LO, :, :].rearrange("p a b -> p (a b)"), raw_att,
                                  watt[:, HI, :, :].rearrange("p a b -> p (a b)").bitcast(F32),
                                  ALU.subtract).then_inc(s_att_lo, 1)
                dve.tensor_tensor(rel_c[:, :], raw_rel[:, 2 * P:2 * P + R], raw_rel[:, 2 * P + R:],
                                  ALU.subtract)
                dve.tensor_tensor(raw_rel[:, 0:P], raw_rel[:, 0:P], raw_rel[:, P:2 * P],
                                  ALU.subtract).then_inc(s_rel, 1)
                dve.wait_ge(s_rel, 1)
                dve.tensor_copy(ctx_s[:, 0:P].bitcast(F32R), raw_rel[:, 0:P])
                dve.tensor_scalar(raw_rel[:, P:2 * P], raw_rel[:, 0:P], lanes[:, 0:1], None,
                                  ALU.mult).then_inc(s_rel, 1)
                dve.wait_ge(s_rel, 2)
                dve.scalar_tensor_tensor(out=rel_g[:, :], in0=ctx_s[:, 0:P], scalar=lanes[:, 1:2],
                                         in1=raw_rel[:, P:2 * P], op0=ALU.mult, op1=ALU.add).then_inc(s_rel, 1)

            def norm_a(m, x):
                for i in range(NT):
                    last = dve.bn_stats(stats[:, i, :], x[:, i * P:(i + 1) * P])
                last.then_inc(s_st, 1)
                dve.wait_ge(s_st, m + 1)
                dve.memset(settled[:, :], 0.0)
                for i in range(NT):
                    last = dve.bn_aggr(moments[:, i, :], stats[:, i, :])
                last.then_inc(s_mom, 1)

            def norm_b(m, x, t=None):
                if t is not None:
                    stored = t if isinstance(t, int) and t == B - 1 else t + 1
                    dve.wait_ge(s_out, 16 * stored)
                dve.wait_ge(s_rstd, m + 1)
                wait(dve, s_xnt, m)
                for i in range(NT):
                    last = dve.tensor_scalar(xn[:, i * P:(i + 1) * P], x[:, i * P:(i + 1) * P],
                                             moments[:, i, 0:1], rstd[:, i:i + 1], ALU.subtract, ALU.mult)
                last.then_inc(s_xn, 1)

            def norm_c(m, xt):
                dve.wait_ge(s_xhi, m + 1)
                dve.tensor_tensor(xt[:, LO, :], work[1][:, :], xt[:, HI, :].bitcast(F32),
                                  ALU.subtract).then_inc(s_xlo, 1)

            def run(name, arg, t):
                if name == "prepare":
                    prepare()
                if name == "add1":
                    dve.wait_ge(s_ftok, sum_index(name, t) + 1)
                    dve.wait_ge(s_x, 16 * (t + 1))
                    dve.tensor_tensor(x1[:, :], work[0][:, :], x0[:, :], ALU.add).then_inc(s_sum, 1)
                if name in ("add2", "addlast"):
                    j = 2 * B - 1 if name == "addlast" else sum_index(name, t)
                    dve.wait_ge(s_ftok, j + 1)
                    dve.wait_ge(s_out, 16 * t)
                    if isinstance(t, int) and t < B:
                        dve.wait_ge(s_xnt, ln_index("ln3", t) + 1)
                    dve.tensor_tensor(out_s[:, :], work[0][:, :], (x2 if name == "add2" else x0)[:, :],
                                      ALU.add).then_inc(s_sum, 1)
                if name == "ln2a":
                    dve.wait_ge(s_sum, sum_index("sum1", t) + 1)
                if name == "ln3a":
                    dve.wait_ge(s_x2, t + 1)
                second_batch = isinstance(t, int) and t == 0 and name[:3] == "ln1"
                if second_batch:
                    dve.wait_ge(s_xb, 16)
                elif name == "ln1a":
                    dve.wait_ge(s_x, 16 * (t + 2))
                if name[:2] == "ln":
                    m = ln_index(name, t)
                    x = x2 if second_batch else {"1": x0, "2": x1, "3": x2_of(t)}[name[2]]
                    if name[3] == "a":
                        norm_a(m, x)
                    if name[3] == "b":
                        norm_b(m, x, t if name[2] == "3" else None)
                    if name[3] == "c":
                        norm_c(m, xt2 if name[2] == "3" or second_batch else xt1)
                if name in ("rot1", "rot2"):
                    rotate(int(name[3]) - 1, t)
                if name == "vadd":
                    dve.wait_ge(s_proj, 5 * t + 5)
                    dve.tensor_tensor(v_rows, ctx_p[:, :].rearrange("p (a b) -> p a b", a=NT),
                                      rel_v0[:, None, :].to_broadcast([P, NT, P]), ALU.add).then_inc(s_v, 1)
                if name[:7] == "quarter":
                    for offset, stage_of in ((REST_MAX, maximum_of_rest), (WINDOW, add_window), (PROBS_HI, probs_hi)):
                        u = due(arg, offset, t)
                        if u is not None:
                            stage_of(u, t)
                    g = group_due(arg, GROUP_SUM, t)
                    if g is not None:
                        dve.wait_ge(s_pv, NU * t + GU * (g + 1))
                        if g > 0:
                            dve.wait_ge(s_crel, HG * t + g)
                        taken = dve.tensor_reduce(
                            ctx_s[:, :].rearrange("p (i g a d) -> p g i a d", i=NT, g=HG, d=DH)[:, g],
                            summed.rearrange("p (i a s d) -> p i a d s", i=NT, s=VP, d=DH), AX.X, ALU.add)
                        if g == 0:
                            taken.then_inc(s_cc, 1)
                        else:
                            add_rel(g - 1, HG * t + g, s_cc, t)
                    if group_due(arg, LAST_REL_SUM, t) == HG - 1:
                        add_rel(HG - 1, HG * t + HG, s_rc, t)
                if name == "scale":
                    dve.wait_ge(s_exp, NU * (t + 1))
                    dve.reciprocal(rdenom[:, :], denom[:, :]).then_inc(s_cn, 1)
                    dve.wait_ge(s_rc, t + 1)
                    dve.wait_ge(s_cn, 2 * t + 1)
                    heads = ctx_s[:, :].rearrange("p (c d) -> p c d", d=DH)
                    dve.tensor_tensor(heads, heads, rdenom[:, :, None].to_broadcast([P, NU, DH]),
                                      ALU.mult).then_inc(s_cn, 1)
                if name == "ctxlo":
                    dve.wait_ge(s_chi, t + 1)
                    dve.tensor_tensor(ctx_t(t)[:, LO, :], work[0][:, :], ctx_t(t)[:, HI, :].bitcast(F32),
                                      ALU.subtract).then_inc(s_clo, 1)
                if name == "attsum":
                    dve.wait_ge(s_o, t + 1)
                    dve.tensor_tensor(x2_of(t)[:, :], work[1][:, :], x1[:, :], ALU.add).then_inc(s_x2, 1)

            def add_rel(g, sums, semaphore, t):
                dve.wait_ge(s_cc, sums)
                dve.wait_ge(s_crel, HG * t + g + 1)
                part = ctx_s[:, :].rearrange("p (i g c) -> p g i c", i=NT, g=HG)[:, g]
                dve.scalar_tensor_tensor(out=part, in0=part, scalar=1.0 / PSCALE,
                                         in1=rel_sum.rearrange("p (i c) -> p i c", i=NT),
                                         op0=ALU.mult, op1=ALU.add).then_inc(semaphore, 1)

            def maximum_of_rest(u, t):
                if u % NT == 0:
                    return
                c = column(u // NT, u % NT)
                dve.wait_ge(s_sc, NU * t + u + 1)
                dve.tensor_reduce(negmax[:, c:c + 1], work[u % 2][:, 0:u % NT * P - R], AX.X,
                                  ALU.min).then_inc(s_rest, 1)

            def add_window(u, t):
                h, i = u // NT, u % NT
                c = column(h, i)
                lo = R if i == 0 else 0
                win = work[u % 2][:, i * P - R + lo:(i + 1) * P]
                if i == 0:
                    wait(dve, s_max, NU * t + u)
                    dve.wait_ge(s_sc, NU * t + u + 1)
                    loads = len(range(h % 3, H, 3))
                    dve.wait_ge(s_z[h % 3], 16 * loads * t + 16 * (h // 3 + 1))
                else:
                    dve.wait_ge(s_rest, (NT - 1) * (H * t + h) + i)
                dve.memset(settled[:, :], 0.0)
                dve.tensor_tensor_reduce(win, win, rel_win[:, h % 3, i, lo:W], 1.0,
                                         3e38 if i == 0 else negmax[:, c:c + 1], ALU.add, ALU.min,
                                         negmax[:, c:c + 1]).then_inc(s_max, 1)

            def probs_hi(u, t):
                h, i = u // NT, u % NT
                dve.wait_ge(s_exp, NU * t + u + 1)
                if u >= PROBS_16:
                    dve.wait_ge(s_pt, NU * t + u + 1 - PROBS_16)
                dve.tensor_copy(probs_16[:, u % PROBS_16, HI, 0:(i + 1) * P],
                                probs[:, h % 2, R + i * L:R + i * L + (i + 1) * P]).then_inc(s_phi, 1)

            def rotate(i, t):
                if i == 0:
                    wait(dve, s_pt, NU * t)
                    for b in range(2):
                        wait(dve, s_pst[b], 16 * (H // 2) * t)
                    if isinstance(t, int) and t == 0:
                        dve.wait_ge(s_wsplit_lo, 2 * E)
                a, b, bank_a, bank_b, scale = ((Q1, Q2, work[0], ctx_p, QSCALE), (K1, K2, work[1], work[2], 1.0))[i]
                dve.wait_ge(s_proj, 5 * t + 2 * i + 1)
                dve.scalar_tensor_tensor(out=a, in0=bank_a[:, :], scalar=scale, in1=cos_s[:, :],
                                         op0=ALU.mult, op1=ALU.mult).then_inc(s_rope, 1)
                dve.wait_ge(s_proj, 5 * t + 2 * i + 2)
                dve.scalar_tensor_tensor(out=b, in0=bank_b[:, :], scalar=scale, in1=sin_s[:, :],
                                         op0=ALU.mult, op1=ALU.mult).then_inc(s_rope, 1)
                dve.wait_ge(s_rope, 6 * t + 3 * i + 2)
                if i == 0:
                    dve.tensor_tensor(a, a, b, ALU.add).then_inc(s_rope, 1)
                else:
                    dve.scalar_tensor_tensor(out=a, in0=a, scalar=rel_k0[:, 0:1], in1=b,
                                             op0=ALU.add, op1=ALU.add).then_inc(s_rope, 1)

            whole_program(dve, chunk, run, prologue, split_expert)

        @block.gpsimd
        def _(pool):
            def lo(n_pass, k):
                n = CH * n_pass + k
                pool.wait_ge(s_hhi, n + 1)
                pool.tensor_tensor(hid_lo[:, k % 2, :], hid[:, k % HB, :], hid_hi[:, k % 2, :].bitcast(F32),
                                   ALU.subtract).then_inc(s_hlo, 1)

            def chunk(part, n_pass, k, second, ln, led):
                j = behind(part, HID_LO, k, led)
                if j is not None:
                    lo(*before(n_pass, k, j))

            def split_expert(e, piece):
                if piece == 2:
                    return
                w = (wg, wu)[piece]
                pool.wait_ge(s_wsplit_hi, 3 * e + piece + 1)
                pool.tensor_tensor(w[:, LO, e, :], stage[e % 2][:, piece * F:(piece + 1) * F],
                                   w[:, HI, e, :].bitcast(F32), ALU.subtract).then_inc(s_wsplit_lo, 1)

            def prologue():
                pool.wait_ge(s_half, 1)
                norm(0)

            def norm(m):
                pool.wait_ge(s_mom, m + 1)
                pool.tensor_tensor(var_eps[:, :], moments[:, :, 1], eps[:, :], ALU.add).then_inc(s_ve, 1)
                pool.wait_ge(s_ve, m + 1)
                pool.tensor_tensor(rstd[:, :], var_eps[:, :], minus_half[:, :], ALU.pow).then_inc(s_rstd, 1)

            def run(name, arg, t):
                if name in ("ln1a", "ln2a", "ln3a"):
                    norm(ln_index(name, t))
                if name in ("qhi", "khi"):
                    i = int(name == "khi")
                    pool.wait_ge(s_qkhi, 2 * t + i + 1)
                    pool.tensor_tensor(qk_r[:, 2 * i + 1, :], (Q1, K1)[i], qk[:, 2 * i, :],
                                       ALU.subtract).then_inc(s_qklo, 1)

                if name in ("vsplit1", "vsplit2"):
                    n = int(name[6]) - 1
                    pool.wait_ge(s_vhi, 2 * t + n + 1)
                    out = v_rows if n == 0 else v_b[:, 2, :, :]
                    pool.tensor_tensor(out, v_rows, v_b[:, n, :, :], ALU.subtract).then_inc(s_v, 1)
                u = due(arg, PROBS_LO, t) if name[:7] == "quarter" else None
                if u is not None:
                    h, i = u // NT, u % NT
                    cols = (i + 1) * P
                    pool.wait_ge(s_phi, NU * t + u + 1)
                    pool.tensor_tensor(probs_16[:, u % PROBS_16, LO, 0:cols],
                                       probs[:, h % 2, R + i * L:R + i * L + cols],
                                       probs_16[:, u % PROBS_16, HI, 0:cols], ALU.subtract).then_inc(s_plo, 1)

            whole_program(pool, chunk, run, prologue, split_expert)


_OUT = ((8, 512, 128), "float32")


def kernel(**inputs):
    import numpy as np
    import concourse.bacc as bacc
    from concourse import mybir
    from concourse.bass_utils import run_bass_kernel_spmd

    x = np.ascontiguousarray(inputs["L0_attn_x"])
    rel = np.asarray(inputs["L0_attn_rel_emb"])
    P, L, H, DH, R, HQ = 128, x.shape[1], 16, 8, 32, 4
    f32 = np.float32

    def dh_major(w):
        return np.asarray(w).reshape(H, DH, P).transpose(1, 0, 2)

    def swapped(w):
        return dh_major(w).reshape(DH // 2, 2, H, P)[:, ::-1].reshape(DH, H, P)

    order = np.array([HQ * (n % HQ) + n // HQ for n in range(H)])
    heads = np.asarray(inputs["L0_attn_w_v"]).reshape(H, DH, P)[order]
    w_o = np.asarray(inputs["L0_attn_w_o"]).reshape(P, H, DH)[:, order].reshape(P, P)
    watt = np.stack([m.reshape(P, P).T for m in (
        dh_major(inputs["L0_attn_w_q"]), swapped(inputs["L0_attn_w_q"]),
        dh_major(inputs["L0_attn_w_k"]), swapped(inputs["L0_attn_w_k"]), heads, w_o)], axis=1)

    rel_g, rel_g0 = np.zeros((HQ, 4, DH, HQ, R), rel.dtype), np.zeros((HQ, 4, DH, HQ, R), rel.dtype)
    rel_c, rel_c0 = np.zeros((HQ, R, HQ, DH), rel.dtype), np.zeros((HQ, R, HQ, DH), rel.dtype)
    for a in range(HQ):
        rel_g[a, :, :, a, :] = rel[1:R + 1].T
        rel_g0[a, :, :, a, :] = rel[0][:, None]
        rel_c[a, :, a, :] = rel[1:R + 1]
        rel_c0[a, :, a, :] = rel[0]

    inv_freq = 1.0 / 10000.0 ** (np.arange(0, DH, 2, dtype=f32) / DH)
    angle = np.outer(inv_freq.astype(f32), np.arange(L, dtype=f32)).astype(f32)
    cos = np.repeat(np.cos(angle.astype(np.float64)), 2, axis=0)
    sin = np.repeat(np.sin(angle.astype(np.float64)), 2, axis=0) * np.tile([-1.0, 1.0], DH // 2)[:, None]
    i, w = np.arange(P)[:, None], np.arange(P + R)[None, :]
    window = np.where(w > i + R, 1e30, 0.0)
    lanes = np.tile(np.repeat([[0.0, 1.0], [1.0, -1.0], [0.0, 1.0], [1.0, -1.0]], DH, axis=0), (HQ, 1))

    arrays = {
        "x": x, "wg": inputs["L0_ffn_Wg"], "wu": inputs["L0_ffn_Wu"], "wd": inputs["L0_ffn_Wd"],
        "watt": watt.reshape(P, -1), "rel_g": rel_g.reshape(P, P), "rel_g0": rel_g0.reshape(P, P),
        "rel_c": rel_c.reshape(P, R), "rel_c0": rel_c0.reshape(P, R),
        "rel_k0": np.repeat(rel[0], H)[:, None], "rel_v0": np.tile(rel[0], (P, H)),
        "cos": np.repeat(cos, H, axis=0).astype(f32), "sin": np.repeat(sin, H, axis=0).astype(f32),
        "window": window.astype(f32), "ident": np.eye(P, dtype=f32), "lanes": lanes.astype(f32),
    }
    nc = bacc.Bacc("TRN2", target_bir_lowering=False, num_devices=1)
    given, args = {}, []
    for name, a in arrays.items():
        a = np.ascontiguousarray(a)
        given[f"in_{name}"] = a
        args.append(nc.dram_tensor(f"in_{name}", a.shape, mybir.dt.from_np(a.dtype), kind="ExternalInput").ap())
    args.append(nc.dram_tensor("out", _OUT[0], mybir.dt.float32, kind="ExternalOutput").ap())
    macaron_kernel(nc, *args)
    return run_bass_kernel_spmd(nc, [given], core_ids=[0]).results[0]["out"]
```
